# Optimizing a Trainium2 kernel written in Bass

```python
import numpy as np
import jax
import jax.numpy as jnp

def _softmax(x, axis=-1):
    return jax.nn.softmax(x, axis=axis)

def _gelu(x):
    return jax.nn.gelu(x, approximate=True)

def _silu(x):
    return jax.nn.silu(x)

def _sigmoid(x):
    return jax.nn.sigmoid(x)

def _layernorm(x, axis=-1, eps=1e-05):
    m = jnp.mean(x, axis=axis, keepdims=True)
    v = jnp.var(x, axis=axis, keepdims=True)
    return (x - m) / jnp.sqrt(v + eps)

def _scatter_add(tgt, idx, src, axis=0):
    return tgt.at[idx].add(src)

def _segment_sum(src, seg, n):
    return jax.ops.segment_sum(src, seg, n)
kernel_name = 'mk_adj_resnorm_d2_adj_r2_5b0937'

def setup_inputs(seed: int=0):
    np.random.seed(seed)
    _w = jnp.asarray

    def _rec_inputs():
        import jax
        import jax.numpy as jnp
        _gk = jax.random.key(seed)
        x = -0.0003929 + 0.9999 * jax.random.normal(jax.random.fold_in(_gk, 1), (16, 512, 128), jnp.float32)
        _a = jax.random.bernoulli(jax.random.fold_in(_gk, 2), 0.03125, (512, 512))
        _a = jnp.logical_or(_a, jnp.swapaxes(_a, -1, -2))
        _a = jnp.logical_or(_a, jnp.eye(512, dtype=bool))
        _af = _a.astype(jnp.float32)
        _af = _af * jax.random.uniform(jax.random.fold_in(_gk, 3), (512, 512), jnp.float32, 0.05, 1)
        adj = _af
        return (x, adj)
    x, adj = _rec_inputs()

    def _L0_gnn_setup():
        import jax, jax.numpy as jnp
        import numpy as np
        EPS = 1e-05

        def _batchnorm(x, gamma, beta):
            mu = jnp.mean(x, axis=0)
            var = jnp.var(x, axis=0)
            return (x - mu) * jax.lax.rsqrt(var + EPS) * gamma + beta
        key = jax.random.key(seed)
        ks = jax.random.split(key, 4)
        b, n, d, h, o = (32, 1024, 128, 256, 128)
        features = jax.random.normal(ks[0], (b, n, d), dtype=jnp.float32)
        A = jax.random.uniform(ks[1], (n, n), dtype=jnp.float32)
        lim1 = float(np.sqrt(6.0 / (d + h)))
        W1 = jax.random.uniform(ks[2], (h, d), minval=-lim1, maxval=lim1, dtype=jnp.float32)
        b1 = jnp.zeros((h,), jnp.float32)
        lim2 = float(np.sqrt(6.0 / (h + o)))
        W2 = jax.random.uniform(ks[3], (o, h), minval=-lim2, maxval=lim2, dtype=jnp.float32)
        b2 = jnp.zeros((o,), jnp.float32)
        g1 = jnp.ones((h,), jnp.float32)
        be1 = jnp.zeros((h,), jnp.float32)
        g2 = jnp.ones((o,), jnp.float32)
        be2 = jnp.zeros((o,), jnp.float32)
        return {'features': features, 'A': A, 'W1': W1, 'b1': b1, 'g1': g1, 'be1': be1, 'W2': W2, 'b2': b2, 'g2': g2, 'be2': be2}
    _L0_gnn_all = _L0_gnn_setup()
    _L0_gnn_in = {k: v for k, v in _L0_gnn_all.items() if k in ('W1', 'b1', 'g1', 'be1', 'W2', 'b2', 'g2', 'be2')}
    del _L0_gnn_all

    def _L1_gnn_setup():
        import jax, jax.numpy as jnp
        import numpy as np
        N_STEPS = 8
        SPATIAL_SCALE = 1.0
        key = jax.random.key(seed)
        ks = jax.random.split(key, 6)
        B, N, D = (32, 512, 128)
        x = jax.random.normal(ks[0], (B, N, D), dtype=jnp.float32)
        adj_mx = jax.random.uniform(ks[1], (N, N), dtype=jnp.float32) / N
        alpha_train = jnp.ones((N,), dtype=jnp.float32)
        w = jnp.eye(D, dtype=jnp.float32) + 0.01 * jax.random.normal(ks[2], (D, D), dtype=jnp.float32)
        d = jax.random.uniform(ks[3], (D,), dtype=jnp.float32)
        fc_in_w = jax.random.normal(ks[4], (D, D), dtype=jnp.float32) * (1.0 / np.sqrt(D))
        fc_in_b = jnp.zeros((D,), dtype=jnp.float32)
        return {'x': x, 'adj_mx': adj_mx, 'alpha_train': alpha_train, 'w': w, 'd': d, 'fc_in_w': fc_in_w, 'fc_in_b': fc_in_b, 'vt': 0}
    _L1_gnn_all = _L1_gnn_setup()
    _L1_gnn_in = {k: v for k, v in _L1_gnn_all.items() if k in ('alpha_train', 'w', 'd', 'fc_in_w', 'fc_in_b')}
    del _L1_gnn_all
    return {'x': x, 'adj': adj, 'L0_gnn_W1': _L0_gnn_in['W1'], 'L0_gnn_b1': _L0_gnn_in['b1'], 'L0_gnn_g1': _L0_gnn_in['g1'], 'L0_gnn_be1': _L0_gnn_in['be1'], 'L0_gnn_W2': _L0_gnn_in['W2'], 'L0_gnn_b2': _L0_gnn_in['b2'], 'L0_gnn_g2': _L0_gnn_in['g2'], 'L0_gnn_be2': _L0_gnn_in['be2'], 'L1_gnn_alpha_train': _L1_gnn_in['alpha_train'], 'L1_gnn_w': _L1_gnn_in['w'], 'L1_gnn_d': _L1_gnn_in['d'], 'L1_gnn_fc_in_w': _L1_gnn_in['fc_in_w'], 'L1_gnn_fc_in_b': _L1_gnn_in['fc_in_b']}

def reference(x, adj, L0_gnn_W1, L0_gnn_b1, L0_gnn_g1, L0_gnn_be1, L0_gnn_W2, L0_gnn_b2, L0_gnn_g2, L0_gnn_be2, L1_gnn_alpha_train, L1_gnn_w, L1_gnn_d, L1_gnn_fc_in_w, L1_gnn_fc_in_b):
    import jax
    import jax.numpy as jnp

    def _L0_gnn_ref(features, A, W1, b1, g1, be1, W2, b2, g2, be2):
        import jax, jax.numpy as jnp
        import numpy as np
        EPS = 1e-05

        def _batchnorm(x, gamma, beta):
            mu = jnp.mean(x, axis=0)
            var = jnp.var(x, axis=0)
            return (x - mu) * jax.lax.rsqrt(var + EPS) * gamma + beta
        b, n, d = features.shape
        A_norm = A + jnp.eye(n, dtype=A.dtype)
        deg = jnp.sum(A_norm, axis=0) + jnp.sum(A_norm, axis=1) - jnp.diagonal(A_norm)
        dinv = jax.lax.rsqrt(deg)
        A_hat = A_norm * dinv[:, None] * dinv[None, :]
        agg = jnp.einsum('nm,bmd->bnd', A_hat, features)
        x = agg.reshape(-1, d)
        h = jax.nn.relu(_batchnorm(x @ W1.T + b1, g1, be1))
        out = h @ W2.T + b2
        out = _batchnorm(out, g2, be2)
        return out.reshape(b, n, -1)

    def _L1_gnn_ref(x, adj_mx, alpha_train, w, d, fc_in_w, fc_in_b, vt):
        import jax, jax.numpy as jnp
        import numpy as np
        N_STEPS = 8
        SPATIAL_SCALE = 1.0
        x0 = jax.lax.stop_gradient(x)
        h = jnp.einsum('bnd,ed->bne', x, fc_in_w) + fc_in_b
        alph = jax.nn.sigmoid(alpha_train)[:, None]
        d_clamped = jnp.clip(d, 0.0, 1.0)
        w_eff = w * d_clamped @ w.T
        dt = jnp.float32(SPATIAL_SCALE / N_STEPS)

        def euler_step(h, _):
            ax = jnp.einsum('nm,bmd->bnd', adj_mx, h)
            f = alph * 0.5 * (ax - h) + h @ w_eff - h + x0
            return (h + dt * f, None)
        h, _ = jax.lax.scan(euler_step, h, None, length=N_STEPS)
        return h
    x = _layernorm(x + _L0_gnn_ref(x, adj, L0_gnn_W1, L0_gnn_b1, L0_gnn_g1, L0_gnn_be1, L0_gnn_W2, L0_gnn_b2, L0_gnn_g2, L0_gnn_be2), axis=-1)
    x = _layernorm(x + _L1_gnn_ref(x, adj, L1_gnn_alpha_train, L1_gnn_w, L1_gnn_d, L1_gnn_fc_in_w, L1_gnn_fc_in_b, 0), axis=-1)
    return x

_drawn_inputs = setup_inputs


def setup_inputs(seed=0):
    import zlib

    import numpy as np

    out = dict(_drawn_inputs(seed))
    spreads = {'L0_gnn_b1': (0.0, 0.1),
     'L0_gnn_g1': (1.0, 0.2),
     'L0_gnn_be1': (0.0, 0.1),
     'L0_gnn_b2': (0.0, 0.1),
     'L0_gnn_g2': (1.0, 0.2),
     'L0_gnn_be2': (0.0, 0.1),
     'L1_gnn_alpha_train': (1.0, 0.2),
     'L1_gnn_fc_in_b': (0.0, 0.1)}
    factors = {}
    for name, (base, spread) in spreads.items():
        noise = np.random.default_rng([zlib.crc32(name.encode()), seed]).standard_normal(out[name].shape)
        drawn = base * np.exp(spread * noise) if base else spread * noise
        out[name] = jnp.asarray(drawn.astype(out[name].dtype))
    for name, factor in factors.items():
        out[name] = (out[name] * factor).astype(out[name].dtype)
    return out
```

```python
from contextlib import ExitStack
from math import comb

import concourse.bass as bass
from concourse import mybir

F32 = mybir.dt.float32
F32R = mybir.dt.float32r
ALU = mybir.AluOpType
ACT = mybir.ActivationFunctionType
AX = mybir.AxisListType


P = 128
EPS = 1e-5
STEPS = 8
DT = 1.0 / STEPS


def gnn_kernel(nc, x, adj, W1, b1, g1, be1, W2, b2, g2, be2, alpha, w, d, fin_w, fin_b, out):
    B, N, D = x.shape
    H = W1.shape[0]
    T = N // P
    FH = H // P
    GB = 4
    NG = B // GB
    assert D == P and T == 4 and FH == 2 and B % GB == 0 and N == 512

    x_v = x.rearrange("b (p t) d -> b p (t d)", t=T)
    out_v = out.rearrange("b (p t) d -> p b t d", t=T)
    adj_v = adj.rearrange("(p t) m -> p t m", t=T)

    with ExitStack() as ctx:
        base = nc.sbuf_base
        base += -base % 64
        used = {}

        def at(name, kb, shape, dt=F32):
            size = 4
            for n in shape[1:]:
                size *= n
            used[name] = (kb, kb + size / 1024)
            return nc.alloc_sbuf_tensor_at(name, shape, dt, offset=base + int(kb * 1024))

        zT = at("zT", 0, [P, FH, B, N])
        oT = zT[:, 0]
        A2 = at("A2", 0, [P, T, T, P])
        raw_w1 = at("raw_w1", 60, [P, FH, D])
        raw_w2 = at("raw_w2", 61, [P, H])
        raw_w = at("raw_w", 62, [P, D])
        diag_t = at("diag_t", 56, [P, T, P])
        UT_hi = at("UT_hi", 32, [P, 2, 3, N], F32R)
        UT_lo = at("UT_lo", 44, [P, 2, 3, N], F32R)
        x1_hi = at("x1_hi", 56, [P, 2, N], F32R)
        x1_lo = at("x1_lo", 60, [P, 2, N], F32R)
        PT_hi = at("PT_hi", 64, [P, T, N], F32R)
        PT_lo = at("PT_lo", 72, [P, T, N], F32R)
        P2_hi = at("P2_hi", 80, [P, T, N], F32R)
        P2_lo = at("P2_lo", 88, [P, T, N], F32R)
        Ah_hi = at("Ah_hi", 96, [P, T, N], F32R)
        Ah_lo = at("Ah_lo", 104, [P, T, N], F32R)
        P3_hi = at("P3_hi", 96, [P, T, N], F32R)
        P3_lo = at("P3_lo", 104, [P, T, N], F32R)
        Pn_hi = at("Pn_hi", 112, [P, T, T, P], F32R)
        Pn_lo = at("Pn_lo", 120, [P, T, T, P], F32R)
        Z2_hi = at("Z2_hi", 112, [P, T, GB, D], F32R)
        Z2_lo = at("Z2_lo", 120, [P, T, GB, D], F32R)
        X_hi = at("X_hi", 128, [P, 2, N], F32R)
        X_lo = at("X_lo", 132, [P, 2, N], F32R)
        ag_hi = at("ag_hi", 136, [P, 2, N], F32R)
        ag_lo = at("ag_lo", 140, [P, 2, N], F32R)
        A_n = at("A_n", 144, [P, T, N])
        h_32 = at("h_32", 128, [P, 2, FH, N])
        h_hi = at("h_hi", 136, [P, 2, FH, N], F32R)
        h_lo = at("h_lo", 144, [P, 2, FH, N], F32R)
        V_hi = at("V_hi", 128, [P, T, GB * D], F32R)
        V_lo = at("V_lo", 136, [P, T, GB * D], F32R)
        Z1 = at("Z1", 144, [P, T, GB, D])
        Pn_32 = at("Pn_32", 152, [P, T, T, P])
        Z0 = at("Z0", 152, [P, T, GB, D])
        X = at("X", 160, [P, 4, N])
        Rp = at("Rp", 168, [P, STEPS + 1, D])
        g_row = at("g_row", 172.5, [P, 3, 3 * D])
        G_32 = at("G_32", 177, [P, 3, 3, D])
        Z2 = at("Z2", 168, [P, 2, T, D])
        V_32 = at("V_32", 172, [P, 2, GB * D])
        y_out = at("y_out", 176, [P, 2, GB, D])
        G_hi = at("G_hi", 181.5, [P, 3, 3, D], F32R)
        G_lo = at("G_lo", 186, [P, 3, 3, D], F32R)
        ZB = at("ZB", 190.5, [P, T, 3 * D])
        W1_hi = at("W1_hi", 196.5, [P, H], F32R)
        W1_lo = at("W1_lo", 197.5, [P, H], F32R)
        W2_hi = at("W2_hi", 198.5, [P, FH, D], F32R)
        W2_lo = at("W2_lo", 199.5, [P, FH, D], F32R)
        y_T = at("y_T", 196.5, [P, 2, N])
        ident = at("ident", 200.5, [P, P])
        raw_f = at("raw_f", 201, [P, D])
        vec = at("vec", 201.5, [P, P])
        wT = at("wT", 202, [P, D])
        wTd = at("wTd", 202.5, [P, D])
        b_bc = at("b_bc", 203, [P, P])
        g_tmp = at("g_tmp", 203.5, [P, D])
        vecT = at("vecT", 204, [P, 16])
        st1 = at("st1", 204.25, [P, FH, B, 6])
        st2 = at("st2", 205, [P, B, 6])
        ones_c = at("ones_c", 205.5, [P, 2])
        small = at("small", 205.625, [P, 64])
        st_x = at("st_x", 206, [P, T, 6])
        st_y = at("st_y", 206.25, [P, GB, 6])
        c_hi = at("c_hi", 206.5, [P, T, 2], F32R)
        c_lo = at("c_lo", 206.5625, [P, T, 2], F32R)
        small2 = at("small2", 206.75, [P, 64])
        assert base + 207 * 1024 <= nc.sbuf_usable_end

        B1, G1, BE1, B2, G2, BE2, DV, FB = 0, 2, 4, 6, 7, 8, 9, 10
        col = lambda k, n=T: small[:, k:k + n]
        rs, cs, dg, deg, sd, dinv, al, c_n, c_d, al_in = (col(4 * i) for i in range(10))
        mv1, v1e, rstd1, s1, t1 = col(40, 4), col(44, 2), col(46, 2), col(48, 2), col(50, 2)
        mv2, v2e, rstd2, s2, t2 = col(52, 2), col(54, 1), col(55, 1), col(56, 1), col(57, 1)
        c1, d_cl, eps_t = col(58, 4), col(62, 1), col(63, 1)
        mvx, sdx, rsx = small2[:, 0:8], small2[:, 8:12], small2[:, 12:16]
        mvy, sdy, rsy = small2[:, 16:24], small2[:, 24:28], small2[:, 28:32]
        c2, c2a = small2[:, 32:36], small2[:, 36:40]
        ms = small2[:, 40:44]

        bank = [ctx.enter_context(nc.psum_tensor(f"bank{i}", [P, 512], F32)) for i in range(8)]

        def sem(name):
            return ctx.enter_context(nc.semaphore(name))

        adj_in, vec_in, w_in, w12_in, alpha_in = (sem(n) for n in ("adj_in", "vec_in", "w_in", "w12_in", "alpha_in"))
        x_in = [sem(f"x_in{i}") for i in range(4)]
        out_sent = [sem("out_sent0"), sem("out_sent1")]
        id_zero, id_ready, consts_ready = sem("id_zero"), sem("id_ready"), sem("consts_ready")
        setup_tr, setup_dve, setup_act = sem("setup_tr"), sem("setup_dve"), sem("setup_act")
        R_mm, R_ready = sem("R_mm"), sem("R_ready")
        cs_done, A2_ready, Ah_tr, Ah_hi_ready, Ah_ready = (sem(n) for n in (
            "cs_done", "A2_ready", "Ah_tr", "Ah_hi_ready", "Ah_ready"))
        cn_ready, pool_link, Pn_ready = sem("cn_ready"), sem("pool_link"), sem("Pn_ready")
        X_hi_ready, X_split, agg_done, ag_hi_ready, agg_split = (sem(n) for n in (
            "X_hi_ready", "X_split", "agg_done", "ag_hi_ready", "agg_split"))
        z_done, z_stored, bn_link, bn_sq, bn_sd = (sem(n) for n in ("z_done", "z_stored", "bn_link", "bn_sq", "bn_sd"))
        bn1_ready, bn2_ready = sem("bn1_ready"), sem("bn2_ready")
        h_ready, h_hi_ready, h_split, o_done, o_stored = (sem(n) for n in (
            "h_ready", "h_hi_ready", "h_split", "o_done", "o_stored"))
        PT_tr, PT_hi_ready, PT_ready = sem("PT_tr"), sem("PT_hi_ready"), sem("PT_ready")
        P2_mm, P2_hi_ready, P2_ready = sem("P2_mm"), sem("P2_hi_ready"), sem("P2_ready")
        P3_mm, P3_hi_ready, P3_ready = sem("P3_mm"), sem("P3_hi_ready"), sem("P3_ready")
        F_mm, F_evac, g_mm, g_evac = sem("F_mm"), sem("F_evac"), sem("g_mm"), sem("g_evac")
        G_sum, G_hi_ready, G_ready = sem("G_sum"), sem("G_hi_ready"), sem("G_ready")
        c_link, c2_mm, zb_link, ZB_ready = sem("c_link"), sem("c2_mm"), sem("zb_link"), sem("ZB_ready")
        y_ready, y_tr, r_ready, xs_link, x_mom, x_sd, x_rstd, x1_ready, x1_hi_ready, x1_split = (sem(n) for n in (
            "y_ready", "y_tr", "r_ready", "xs_link", "x_mom", "x_sd", "x_rstd", "x1_ready", "x1_hi_ready",
            "x1_split"))
        U_done, U_hi_ready, U_split = sem("U_done"), sem("U_hi_ready"), sem("U_split")
        Z_done, Z_stored, Z2_hi_ready, Z2_split = sem("Z_done"), sem("Z_stored"), sem("Z2_hi_ready"), sem("Z2_split")
        V_done, V_sum, V_hi_ready, V_split = sem("V_done"), sem("V_sum"), sem("V_hi_ready"), sem("V_split")
        F_done, q_ready, ys_link, y_mom, y_sd, y_rstd, out_ready = (sem(n) for n in (
            "F_done", "q_ready", "ys_link", "y_mom", "y_sd", "y_rstd", "out_ready"))

        block = ctx.enter_context(nc.Block())

        LAST = B - 2

        @block.sync
        def _(sp):
            sp.dma_start(A_n[:], adj_v).then_inc(adj_in, 16)
            for s in range(4):
                sp.dma_start(X[:, s], x_v[s]).then_inc(x_in[s], 16)
            with sp.Fori(1, B // 4) as i:
                for s in range(4):
                    sp.wait_ge(X_split, i * 4 + (s - 3))
                    sp.dma_start(X[:, s], x_v[i * 4 + s]).then_inc(x_in[s], 16)
            for s in range(4):
                sp.wait_ge(X_split, B - 3 + s)
                sp.dma_start(X[:, s], x_v[s]).then_inc(x_in[s], 16)
            def send(g):
                for t in range(T):
                    sp.wait_ge(out_ready, g * T + (t + 1))
                    sp.dma_start(out_v[:, bass.ds(g * GB, GB), t, :], y_out[:, t % 2]).then_inc(out_sent[t % 2], 16)

            with sp.Fori(1, NG) as g:
                for s in range(4):
                    sp.wait_ge(U_done, (g * 4 + (s - 3)) * 3)
                    sp.dma_start(X[:, s], x_v[g * 4 + s]).then_inc(x_in[s], 16)
                send(g - 1)
            send(NG - 1)
            for s in range(2):
                sp.wait_ge(out_sent[s], 16 * (NG * T // 2 + 1))

        @block.gpsimd
        def _(pool):
            pool.memset(ident[:], 0.0).then_inc(id_zero, 1)
            pool.memset(vec[:], 0.0).then_inc(id_zero, 1)
            pool.wait_ge(id_zero, 2)
            pool.affine_select(out=ident[:], in_=ident[:], compare_op=ALU.not_equal, fill=1.0, base=0,
                               pattern=[[-1, P]], channel_multiplier=1).then_inc(id_ready, 1)
            pool.memset(ones_c[:], 1.0)
            pool.memset(eps_t, EPS).then_inc(consts_ready, 1)
            link = 0
            pool.wait_ge(adj_in, 16)
            pool.wait_ge(cn_ready, 2)
            for t in range(T):
                last = pool.tensor_scalar(Pn_32[:, t], A_n[:, t].rearrange("p (q u) -> p u q", u=T),
                                          c_n[:, t:t + 1], 1.0, ALU.mult, ALU.mult)
            last.then_inc(pool_link, 1)
            link += 1
            for t in range(T):
                pool.wait_ge(pool_link, link)
                pool.wait_ge(id_ready, 1)
                pool.tensor_scalar(g_tmp[:], ident[:], c_d[:, t:t + 1], 1.0, ALU.mult, ALU.mult).then_inc(pool_link, 1)
                link += 1
                pool.wait_ge(pool_link, link)
                pool.tensor_tensor(Pn_32[:, t, t], Pn_32[:, t, t], g_tmp[:], ALU.add).then_inc(pool_link, 1)
                link += 1
            pool.wait_ge(pool_link, link)
            pool.tensor_copy(Pn_hi[:], Pn_32[:]).then_inc(pool_link, 1)
            link += 1
            pool.wait_ge(pool_link, link)
            pool.tensor_tensor(Pn_lo[:], Pn_32[:], Pn_hi[:].bitcast(F32), ALU.subtract).then_inc(Pn_ready, 1)
            pool.wait_ge(F_evac, 9)
            pool.wait_ge(R_ready, 4)
            for k in range(STEPS):
                for m in range(STEPS - k):
                    coef = DT * comb(m + k, k) + (1.0 if k == 0 and m == 0 else 0.0)
                    src = ident[:] if m == 0 else Rp[:, m]
                    pool.wait_ge(pool_link, link)
                    pool.tensor_scalar(g_tmp[:], src, coef, 1.0, ALU.mult, ALU.mult).then_inc(pool_link, 1)
                    link += 1
                    pool.wait_ge(pool_link, link)
                    dst = G_32[:, k % 3, k // 3]
                    pool.tensor_tensor(dst, dst, g_tmp[:], ALU.add).then_inc(pool_link, 1)
                    link += 1
            pool.wait_ge(pool_link, link)
            pool.tensor_copy(G_hi[:], G_32[:]).then_inc(G_hi_ready, 1)
            pool.wait_ge(G_hi_ready, 1)
            pool.tensor_tensor(G_lo[:], G_32[:], G_hi[:].bitcast(F32), ALU.subtract).then_inc(G_ready, 1)

        @block.scalar
        def _(act):
            act.dma_start(raw_w[:], w).then_inc(w_in, 16)
            act.wait_ge(id_zero, 2)
            for row, v in ((B1, b1), (G1, g1), (BE1, be1)):
                act.dma_start(vec[row:row + FH, :], v.rearrange("(f p) -> f p", p=P)).then_inc(vec_in, 16)
            for row, v in ((B2, b2), (G2, g2), (BE2, be2), (DV, d), (FB, fin_b)):
                act.dma_start(vec[row:row + 1, :], v.rearrange("(a p) -> a p", a=1)).then_inc(vec_in, 16)
            act.dma_start(al_in, alpha.rearrange("(p t) -> p t", t=T)).then_inc(alpha_in, 16)
            act.dma_start(raw_w1[:], W1.rearrange("(f p) d -> p f d", p=P)).then_inc(w12_in, 16)
            act.dma_start(raw_w2[:], W2).then_inc(w12_in, 16)
            act.dma_start(raw_f[:], fin_w).then_inc(w12_in, 16)
            act.wait_ge(alpha_in, 16)
            act.activation(al, al_in, ACT.Sigmoid).then_inc(setup_act, 1)
            act.wait_ge(setup_dve, 10)
            act.activation(sd, deg, ACT.Sqrt).then_inc(setup_act, 1)

            for b in range(2):
                act.wait_ge(x_in[b], 16)
                act.activation(X_hi[:, b], X[:, b], ACT.Copy).then_inc(X_hi_ready, 1)
            act.wait_ge(setup_tr, 3)
            act.activation(W1_hi[:], bank[5][:, 0:H], ACT.Copy).then_inc(setup_act, 1)
            act.activation(W2_hi[:], bank[5][:, H:2 * H], ACT.Copy).then_inc(setup_act, 1)
            act.wait_ge(A2_ready, 1)
            for t in range(T):
                act.wait_ge(Ah_tr, t + 1)
                act.activation(Ah_hi[:, t], bank[t][:], ACT.Copy, scale=dinv[:, t:t + 1]).then_inc(Ah_hi_ready, 1)
            act.sem_inc(z_stored, 4)
            act.wait_ge(setup_dve, 1)

            def layer1(b, s, x_wait, more=True):
                act.wait_ge(agg_done, b + 1)
                act.activation(ag_hi[:, s % 2], bank[s % 2][:], ACT.Copy).then_inc(ag_hi_ready, 1)
                if more:
                    act.wait_ge(x_in[(s + 2) % 4], x_wait)
                    act.activation(X_hi[:, s % 2], X[:, (s + 2) % 4], ACT.Copy).then_inc(X_hi_ready, 1)
                for f in range(FH):
                    act.wait_ge(z_done, b * FH + (f + 1))
                    act.activation(zT[:, f, b, :], bank[2 + FH * (s % 2) + f][:], ACT.Identity,
                                   bias=vecT[:, B1 + f:B1 + f + 1]).then_inc(z_stored, 1)

            with act.Fori(0, B // 4 - 1) as i:
                for s in range(4):
                    layer1(i * 4 + s, s, (i + 1 + (s + 2) // 4) * 16)
            for s in range(4):
                layer1(B - 4 + s, s, B // 4 * 16, more=s < 2)

            for t in range(T):
                act.wait_ge(PT_tr, t + 1)
                act.activation(PT_hi[:, t], bank[t][:], ACT.Copy).then_inc(PT_hi_ready, 1)
            act.wait_ge(bn_sq, 1)
            act.activation(v1e, mv1.rearrange("p (f two) -> p f two", two=2)[:, :, 1], ACT.Sqrt,
                           bias=eps_t).then_inc(bn_sd, 1)
            for m in range(STEPS + 1):
                k = STEPS - m
                act.wait_ge(F_mm, m // 3 + 1)
                act.activation(G_32[:, k % 3, k // 3], bank[4 + m // 3][:, (m % 3) * D:(m % 3 + 1) * D], ACT.Copy,
                               scale=float(comb(STEPS, k))).then_inc(F_evac, 1)
            for t in range(T):
                act.wait_ge(P2_mm, t + 1)
                act.activation(P2_hi[:, t], bank[t][:], ACT.Copy).then_inc(P2_hi_ready, 1)
            for m in range(STEPS + 1):
                k = STEPS - m
                act.wait_ge(g_mm, m // 3 + 1)
                act.activation(g_row[:, k % 3, (k // 3) * D:(k // 3 + 1) * D],
                               bank[4 + m // 3][:, (m % 3) * D:(m % 3 + 1) * D], ACT.Copy,
                               scale=float(comb(STEPS, k))).then_inc(g_evac, 1)

            act.wait_ge(bn1_ready, 1)
            act.sem_inc(o_stored, 2)
            act.wait_ge(Pn_ready, 1)

            def relu(b, s):
                for f in range(FH):
                    act.activation(h_32[:, s, f], zT[:, f, b, :], ACT.Relu, bias=t1[:, f:f + 1],
                                   scale=s1[:, f:f + 1]).then_inc(h_ready, 1)

            def store_o(b, s):
                act.wait_ge(o_done, b + 1)
                act.activation(oT[:, b, :], bank[6 + s][:], ACT.Identity,
                               bias=vecT[:, B2:B2 + 1]).then_inc(o_stored, 1)

            relu(0, 0)
            relu(1, 1)
            with act.Fori(0, B // 2 - 1) as i:
                for s in range(2):
                    b = i * 2 + s
                    store_o(b, s)
                    relu(b + 2, s)
            for s in range(2):
                store_o(B - 2 + s, s)

            for t in range(T):
                act.wait_ge(P3_mm, t + 1)
                act.activation(P3_hi[:, t], bank[t][:], ACT.Copy).then_inc(P3_hi_ready, 1)
            act.wait_ge(bn_sq, 2)
            act.activation(v2e, mv2[:, 1:2], ACT.Sqrt, bias=eps_t).then_inc(bn_sd, 1)
            act.wait_ge(bn2_ready, 1)

            def affine(c, s):
                act.activation(y_T[:, s % 2], oT[:, c, :], ACT.Identity, bias=t2, scale=s2).then_inc(y_ready, 1)

            def root(c):
                act.wait_ge(x_mom, c + 1)
                act.activation(sdx, mvx.rearrange("p (t two) -> p t two", two=2)[:, :, 1], ACT.Sqrt,
                               bias=eps_t).then_inc(x_sd, 1)

            def x1_high(c, s):
                act.wait_ge(x1_ready, c + 1)
                act.activation(x1_hi[:, s % 2], X[:, s % 4], ACT.Copy).then_inc(x1_hi_ready, 1)

            def u_high(c, s, j):
                act.wait_ge(U_done, c * 3 + (j + 1))
                act.activation(UT_hi[:, s % 2, j], bank[1 + j][:], ACT.Copy).then_inc(U_hi_ready, 1)

            def stage_u(c, s, nxt=True, nxt2=True):
                u_high(c, s, 0)
                if nxt2:
                    affine(c + 2, s)
                if nxt:
                    root(c + 1)
                u_high(c, s, 1)
                u_high(c, s, 2)
                if nxt:
                    x1_high(c + 1, s + 1)

            def stage_z(c, s):
                act.wait_ge(Z_stored, c * T + (T + 2))
                act.activation(Z2_hi[:, :, s % GB, :], Z2[:, s % 2], ACT.Copy).then_inc(Z2_hi_ready, 1)

            def stage_v(g):
                for t in range(T):
                    act.wait_ge(V_sum, g * T + (t + 1))
                    act.activation(V_hi[:, t], V_32[:, t % 2], ACT.Copy).then_inc(V_hi_ready, 1)

            def stage_f(g):
                for t in range(T):
                    act.wait_ge(y_mom, g * T + (t + 1))
                    act.activation(sdy, mvy.rearrange("p (t two) -> p t two", two=2)[:, :, 1], ACT.Sqrt,
                                   bias=eps_t).then_inc(y_sd, 1)

            affine(0, 0)
            affine(1, 1)
            root(0)
            x1_high(0, 0)
            stage_u(0, 0)
            stage_u(1, 1)
            with act.Fori(0, NG - 1) as g:
                for s in range(GB):
                    stage_z(g * GB + s, s)
                    stage_u(g * GB + (s + 2), s + 2)
                stage_v(g)
                stage_f(g)
            g = NG - 1
            for s in range(GB):
                stage_z(g * GB + s, s)
                if s < 2:
                    stage_u(g * GB + s + 2, s + 2, nxt=s < 1, nxt2=False)
            stage_v(g)
            stage_f(g)

        @block.vector
        def _(dve):
            n = 0

            def link(ins):
                nonlocal n
                n += 1
                ins.then_inc(setup_dve, 1)
                dve.wait_ge(setup_dve, n)

            dve.wait_ge(setup_tr, 1)
            link(dve.tensor_copy(vecT[:], bank[6][:, 0:16]))
            link(dve.tensor_scalar(d_cl, vecT[:, DV:DV + 1], 0.0, 1.0, ALU.max, ALU.min))
            dve.wait_ge(setup_tr, 2)
            link(dve.tensor_copy(wT[:], bank[7][:, 0:D]))
            link(dve.tensor_scalar(wTd[:], wT[:], d_cl, None, ALU.mult))
            dve.wait_ge(adj_in, 16)
            dve.wait_ge(id_ready, 1)
            for t in range(T):
                last = dve.tensor_tensor(diag_t[:, t], A_n[:, t].rearrange("p (q u) -> p u q", u=T)[:, t], ident[:],
                                         ALU.mult)
            link(last)
            link(dve.reduce_sum(dg, diag_t[:], AX.X))
            link(dve.reduce_sum(rs, A_n[:], AX.X))
            dve.wait_ge(R_mm, 1)
            dve.tensor_scalar(Rp[:, 1], bank[7][:, 0:D], DT, None, ALU.mult).then_inc(R_ready, 1)
            dve.wait_ge(cs_done, 1)
            link(dve.scalar_tensor_tensor(out=deg, in0=bank[6][:, 0:T], scalar=1.0, in1=rs, op0=ALU.add, op1=ALU.add))
            link(dve.tensor_tensor(cs, deg, dg, ALU.subtract))
            link(dve.tensor_copy(deg, cs))
            dve.wait_ge(R_mm, 2)
            dve.tensor_copy(Rp[:, 2], bank[7][:, 0:D]).then_inc(R_ready, 1)
            dve.wait_ge(setup_act, 2)
            link(dve.reciprocal(dinv, sd))
            for t in range(T):
                last = dve.tensor_scalar(A2[:, t], A_n[:, t].rearrange("p (q u) -> p u q", u=T), dinv[:, t:t + 1],
                                         None, ALU.mult)
            link(last)
            for t in range(T):
                last = dve.scalar_tensor_tensor(out=A2[:, t, t], in0=ident[:], scalar=dinv[:, t:t + 1],
                                                in1=A2[:, t, t], op0=ALU.mult, op1=ALU.add)
            last.then_inc(A2_ready, 1)
            dve.tensor_scalar(c_n, al, DT * 0.5, None, ALU.mult).then_inc(cn_ready, 1)
            dve.tensor_scalar(c_d, al, -DT * 0.5, 1.0 - DT, ALU.mult, ALU.add).then_inc(cn_ready, 1)
            dve.wait_ge(R_mm, 3)
            dve.tensor_copy(Rp[:, 3:5], bank[7][:, 0:2 * D]).then_inc(R_ready, 1)
            for b in range(2):
                dve.wait_ge(X_hi_ready, b + 1)
                dve.tensor_tensor(X_lo[:, b], X[:, b], X_hi[:, b].bitcast(F32), ALU.subtract).then_inc(X_split, 1)
            dve.wait_ge(setup_act, 4)
            link(dve.tensor_tensor(W1_lo[:], bank[5][:, 0:H], W1_hi[:].bitcast(F32), ALU.subtract))
            link(dve.tensor_tensor(W2_lo[:].rearrange("p f d -> p (f d)"), bank[5][:, H:2 * H],
                                   W2_hi[:].rearrange("p f d -> p (f d)").bitcast(F32), ALU.subtract))
            for t in range(T):
                dve.wait_ge(Ah_hi_ready, t + 1)
                dve.scalar_tensor_tensor(out=Ah_lo[:, t], in0=bank[t][:], scalar=dinv[:, t:t + 1],
                                         in1=Ah_hi[:, t].bitcast(F32), op0=ALU.mult,
                                         op1=ALU.subtract).then_inc(Ah_ready, 1)
            dve.wait_ge(R_mm, 4)
            dve.tensor_copy(Rp[:, 5:9], bank[7][:, 0:4 * D]).then_inc(R_ready, 1)
            dve.tensor_scalar(Rp[:, 0], ident[:], 1.0, None, ALU.mult).then_inc(R_ready, 1)
            dve.tensor_scalar(b_bc[:], ident[:], 0.0, vecT[:, FB:FB + 1], ALU.mult, ALU.add).then_inc(R_ready, 1)

            dve.sem_inc(agg_split, 2)

            def layer1(b, s, more=True):
                dve.wait_ge(ag_hi_ready, b + 1)
                dve.tensor_tensor(ag_lo[:, s % 2], bank[s % 2][:], ag_hi[:, s % 2].bitcast(F32),
                                  ALU.subtract).then_inc(agg_split, 1)
                if more:
                    dve.wait_ge(X_hi_ready, b + 3)
                    dve.tensor_tensor(X_lo[:, s % 2], X[:, (s + 2) % 4], X_hi[:, s % 2].bitcast(F32),
                                      ALU.subtract).then_inc(X_split, 1)
                for f in range(FH):
                    dve.wait_ge(z_stored, b * FH + (f + 1 + 4))
                    last = dve.bn_stats(st1[:, f, b, :], zT[:, f, b, :])
                if not more:
                    last.then_inc(bn_link, 1)

            with dve.Fori(0, B // 4 - 1) as i:
                for s in range(4):
                    layer1(i * 4 + s, s)
            for s in range(4):
                layer1(B - 4 + s, s, more=s < 2)

            dve.wait_ge(bn_link, 2)
            for f in range(FH):
                last = dve.bn_aggr(mv1[:, 2 * f:2 * f + 2], st1[:, f].rearrange("p b k -> p (b k)"))
            last.then_inc(bn_sq, 1)
            for t in range(T):
                dve.wait_ge(PT_hi_ready, t + 1)
                dve.tensor_tensor(PT_lo[:, t], bank[t][:], PT_hi[:, t].bitcast(F32), ALU.subtract).then_inc(PT_ready, 1)
            dve.wait_ge(bn_sd, 1)
            dve.reciprocal(rstd1, v1e).then_inc(bn_link, 1)
            dve.wait_ge(bn_link, 3)
            dve.tensor_tensor(s1, rstd1, vecT[:, G1:G1 + FH], ALU.mult).then_inc(bn_link, 1)
            dve.wait_ge(bn_link, 4)
            dve.tensor_tensor(ms[:, 0:FH], mv1.rearrange("p (f two) -> p f two", two=2)[:, :, 0], s1,
                              ALU.mult).then_inc(bn_link, 1)
            dve.wait_ge(bn_link, 5)
            dve.tensor_tensor(t1, vecT[:, BE1:BE1 + FH], ms[:, 0:FH], ALU.subtract).then_inc(bn1_ready, 1)
            dve.wait_ge(Pn_ready, 1)
            dve.reduce_sum(c1, Pn_32[:].rearrange("p t u q -> p t (u q)"), AX.X).then_inc(c_link, 1)
            dve.wait_ge(c_link, 1)
            for two in range(2):
                last = dve.tensor_copy(c_hi[:, :, two], c1)
            last.then_inc(c_link, 1)
            dve.wait_ge(c_link, 2)
            for two in range(2):
                last = dve.tensor_tensor(c_lo[:, :, two], c1, c_hi[:, :, two].bitcast(F32), ALU.subtract)
            last.then_inc(c_link, 1)
            for t in range(T):
                dve.wait_ge(P2_hi_ready, t + 1)
                dve.tensor_tensor(P2_lo[:, t], bank[t][:], P2_hi[:, t].bitcast(F32), ALU.subtract).then_inc(P2_ready, 1)

            def split_h(b, s):
                dve.wait_ge(h_ready, b * FH + FH)
                dve.tensor_copy(h_hi[:, s], h_32[:, s]).then_inc(h_hi_ready, 1)
                dve.wait_ge(h_hi_ready, b + 1)
                dve.tensor_tensor(h_lo[:, s], h_32[:, s], h_hi[:, s].bitcast(F32), ALU.subtract).then_inc(h_split, 1)

            def stats_o(b, s, last=False):
                dve.wait_ge(o_stored, b + 3)
                ins = dve.bn_stats(st2[:, b, :], oT[:, b, :])
                if last:
                    ins.then_inc(bn_link, 1)

            split_h(0, 0)
            split_h(1, 1)
            with dve.Fori(0, B // 2 - 1) as i:
                for s in range(2):
                    b = i * 2 + s
                    stats_o(b, s)
                    split_h(b + 2, s)
            for s in range(2):
                stats_o(B - 2 + s, s, last=s == 1)
            dve.wait_ge(bn_link, 6)
            dve.bn_aggr(mv2, st2[:].rearrange("p b k -> p (b k)")).then_inc(bn_sq, 1)
            for t in range(T):
                dve.wait_ge(P3_hi_ready, t + 1)
                dve.tensor_tensor(P3_lo[:, t], bank[t][:], P3_hi[:, t].bitcast(F32), ALU.subtract).then_inc(P3_ready, 1)
            dve.wait_ge(bn_sd, 2)
            dve.reciprocal(rstd2, v2e).then_inc(bn_link, 1)
            dve.wait_ge(bn_link, 7)
            dve.tensor_tensor(s2, rstd2, vecT[:, G2:G2 + 1], ALU.mult).then_inc(bn_link, 1)
            dve.wait_ge(bn_link, 8)
            dve.tensor_tensor(ms[:, 2:3], mv2[:, 0:1], s2, ALU.mult).then_inc(bn_link, 1)
            dve.wait_ge(bn_link, 9)
            dve.tensor_tensor(t2, vecT[:, BE2:BE2 + 1], ms[:, 2:3], ALU.subtract).then_inc(bn2_ready, 1)
            dve.wait_ge(c2_mm, 1)
            dve.tensor_copy(c2, bank[4][:].rearrange("p (t k) -> p t k", k=P)[:, :, 0]).then_inc(zb_link, 1)
            dve.wait_ge(g_evac, 9)
            dve.wait_ge(zb_link, 1)
            for t in range(T):
                last = dve.scalar_tensor_tensor(out=ZB[:, t], in0=g_row[:, 1], scalar=c1[:, t:t + 1],
                                                in1=g_row[:, 0], op0=ALU.mult, op1=ALU.add)
            last.then_inc(zb_link, 1)
            dve.wait_ge(zb_link, 2)
            for t in range(T):
                last = dve.scalar_tensor_tensor(out=ZB[:, t], in0=g_row[:, 2], scalar=c2[:, t:t + 1],
                                                in1=ZB[:, t], op0=ALU.mult, op1=ALU.add)
            last.then_inc(ZB_ready, 1)
            dve.wait_ge(ZB_ready, 1)
            dve.sem_inc(r_ready, 1)
            dve.sem_inc(U_split, 3)
            dve.sem_inc(Z_stored, 2)
            dve.sem_inc(q_ready, 1)
            for s in range(2):
                dve.sem_inc(out_sent[s], 16)

            def moments(c, s, x_wait):
                dve.wait_ge(x_in[s % 4], x_wait)
                dve.wait_ge(y_tr, c + 1)
                dve.tensor_tensor(X[:, s % 4], X[:, s % 4], bank[0][:], ALU.add).then_inc(r_ready, 1)
                dve.wait_ge(r_ready, c + 2)
                for t in range(T):
                    last = dve.bn_stats(st_x[:, t], X[:, s % 4, t * D:(t + 1) * D])
                last.then_inc(xs_link, 1)
                dve.wait_ge(xs_link, c + 1)
                dve.nop(nofuse=True)
                for t in range(T):
                    last = dve.bn_aggr(mvx[:, 2 * t:2 * t + 2], st_x[:, t])
                last.then_inc(x_mom, 1)

            def normalize(c, s):
                dve.wait_ge(x_sd, c + 1)
                dve.reciprocal(rsx, sdx).then_inc(x_rstd, 1)
                dve.wait_ge(x_rstd, c + 1)
                for t in range(T):
                    last = dve.tensor_scalar(X[:, s % 4, t * D:(t + 1) * D], X[:, s % 4, t * D:(t + 1) * D],
                                             mvx[:, 2 * t:2 * t + 1], rsx[:, t:t + 1], ALU.subtract, ALU.mult)
                last.then_inc(x1_ready, 1)

            def x1_low(c, s):
                dve.wait_ge(x1_hi_ready, c + 1)
                dve.tensor_tensor(x1_lo[:, s % 2], X[:, s % 4], x1_hi[:, s % 2].bitcast(F32),
                                  ALU.subtract).then_inc(x1_split, 1)

            def u_low(c, s, j):
                dve.wait_ge(U_hi_ready, c * 3 + (j + 1))
                dve.tensor_tensor(UT_lo[:, s % 2, j], bank[1 + j][:], UT_hi[:, s % 2, j].bitcast(F32),
                                  ALU.subtract).then_inc(U_split, 1)

            def stage_u(c, s, x_wait=None):
                u_low(c, s, 0)
                if x_wait is not None:
                    moments(c + 1, s + 1, x_wait)
                u_low(c, s, 1)
                if x_wait is not None:
                    normalize(c + 1, s + 1)
                u_low(c, s, 2)
                if x_wait is not None:
                    x1_low(c + 1, s + 1)

            def stage_z(c, s):
                for t in range(T):
                    dve.wait_ge(Z_done, c * T + (t + 1))
                    src = bank[4 + t % 2]
                    dve.tensor_tensor(Z0[:, t, s % GB], src[:, 0:D], ZB[:, t, 0:D], ALU.add)
                    dve.tensor_tensor(Z1[:, t, s % GB], src[:, D:2 * D], ZB[:, t, D:2 * D], ALU.add)
                    dve.tensor_tensor(Z2[:, s % 2, t], src[:, 2 * D:3 * D], ZB[:, t, 2 * D:3 * D],
                                      ALU.add).then_inc(Z_stored, 1)
                dve.wait_ge(Z2_hi_ready, c + 1)
                dve.tensor_tensor(Z2_lo[:, :, s % GB, :], Z2[:, s % 2], Z2_hi[:, :, s % GB, :].bitcast(F32),
                                  ALU.subtract).then_inc(Z2_split, 1)

            def v_low(g, t):
                dve.wait_ge(V_hi_ready, g * T + (t + 1))
                dve.tensor_tensor(V_lo[:, t], V_32[:, t % 2], V_hi[:, t].bitcast(F32),
                                  ALU.subtract).then_inc(V_split, 1)

            def stage_v(g):
                for t in range(T):
                    if t >= 2:
                        dve.wait_ge(V_split, g * T + (t - 1))
                    dve.wait_ge(V_done, g * T + (t + 1))
                    dve.tensor_tensor(V_32[:, t % 2], bank[6 + t % 2][:], Z1[:, t].rearrange("p s d -> p (s d)"),
                                      ALU.add).then_inc(V_sum, 1)
                    if t:
                        v_low(g, t - 1)
                v_low(g, T - 1)

            def stage_f(g):
                for t in range(T):
                    dve.wait_ge(F_done, g * T + (t + 1))
                    dve.wait_ge(out_sent[t % 2], (g * 2 + (t // 2 + 1)) * 16)
                    yo = y_out[:, t % 2]
                    dve.tensor_tensor(yo.rearrange("p s d -> p (s d)"), bank[6 + t % 2][:],
                                      Z0[:, t].rearrange("p s d -> p (s d)"), ALU.add).then_inc(q_ready, 1)
                    dve.wait_ge(q_ready, g * T + (t + 2))
                    for s in range(GB):
                        last = dve.bn_stats(st_y[:, s], yo[:, s])
                    last.then_inc(ys_link, 1)
                    dve.wait_ge(ys_link, g * T + (t + 1))
                    dve.nop(nofuse=True)
                    for s in range(GB):
                        last = dve.bn_aggr(mvy[:, 2 * s:2 * s + 2], st_y[:, s])
                    last.then_inc(y_mom, 1)
                    dve.wait_ge(y_sd, g * T + (t + 1))
                    dve.reciprocal(rsy, sdy).then_inc(y_rstd, 1)
                    dve.wait_ge(y_rstd, g * T + (t + 1))
                    for s in range(GB):
                        last = dve.tensor_scalar(yo[:, s], yo[:, s], mvy[:, 2 * s:2 * s + 1], rsy[:, s:s + 1],
                                                 ALU.subtract, ALU.mult)
                    last.then_inc(out_ready, 1)

            x2 = B // 4
            moments(0, 0, (x2 + 1) * 16)
            normalize(0, 0)
            x1_low(0, 0)
            stage_u(0, 0, (x2 + 1) * 16)
            stage_u(1, 1, (x2 + 1) * 16)
            with dve.Fori(0, NG - 1) as g:
                for s in range(GB):
                    stage_z(g * GB + s, s)
                    stage_u(g * GB + (s + 2), s + 2, (g + (x2 + 1 + (s + 3) // 4)) * 16)
                stage_v(g)
                stage_f(g)
            g = NG - 1
            for s in range(GB):
                stage_z(g * GB + s, s)
                if s < 2:
                    stage_u(g * GB + s + 2, s + 2, (x2 + NG) * 16 if s < 1 else None)
            stage_v(g)
            stage_f(g)

        @block.tensor
        def _(pe):
            def split_mm(dst, w_hi, w_lo, m_hi, m_lo, first, last):
                pe.matmul(dst, w_hi, m_hi, start=first, stop=False)
                pe.matmul(dst, w_hi, m_lo, start=False, stop=False)
                return pe.matmul(dst, w_lo, m_hi, start=False, stop=last)

            pe.wait_ge(id_ready, 1)
            pe.wait_ge(vec_in, 8 * 16)
            pe.transpose(bank[6][:, 0:P], vec[:], ident[:]).then_inc(setup_tr, 1)
            pe.wait_ge(w_in, 16)
            pe.transpose(bank[7][:, 0:P], raw_w[:], ident[:]).then_inc(setup_tr, 1)
            pe.wait_ge(w12_in, 3 * 16)
            for f in range(FH):
                pe.transpose(bank[5][:, f * P:(f + 1) * P], raw_w1[:, f], ident[:])
            for f in range(FH):
                last = pe.transpose(bank[5][:, H + f * P:H + (f + 1) * P], raw_w2[:, f * P:(f + 1) * P], ident[:])
            last.then_inc(setup_tr, 1)
            pe.wait_ge(setup_dve, 4)
            pe.matmul(bank[7][:, 0:D], wTd[:], wT[:], start=True, stop=True).then_inc(R_mm, 1)
            pe.wait_ge(adj_in, 16)
            pe.wait_ge(consts_ready, 1)
            for u in range(T):
                for t in range(T):
                    last = pe.matmul(bank[6][:, u:u + 1], A_n[:, t].rearrange("p (q u) -> p u q", u=T)[:, u],
                                     ones_c[:, 0:1], start=t == 0, stop=t == T - 1)
            last.then_inc(cs_done, 1)
            pe.wait_ge(R_ready, 1)
            pe.matmul(bank[7][:, 0:D], Rp[:, 1], Rp[:, 1], start=True, stop=True).then_inc(R_mm, 1)
            pe.wait_ge(R_ready, 2)
            pe.matmul(bank[7][:, 0:2 * D], Rp[:, 2], Rp[:, 1:3], start=True, stop=True).then_inc(R_mm, 1)
            pe.wait_ge(A2_ready, 1)
            for u in range(T):
                for t in range(T):
                    last = pe.transpose(bank[u][:, t * P:(t + 1) * P], A2[:, t, u], ident[:])
                last.then_inc(Ah_tr, 1)
            pe.wait_ge(R_ready, 3)
            pe.matmul(bank[7][:, 0:4 * D], Rp[:, 4], Rp[:, 1:5], start=True, stop=True).then_inc(R_mm, 1)

            def aggregate(b, s):
                pe.wait_ge(X_split, b + 1)
                pe.wait_ge(agg_split, b + 1)
                for t in range(T):
                    k = slice(t * D, (t + 1) * D)
                    last = split_mm(bank[s % 2][:], X_hi[:, s % 2, k], X_lo[:, s % 2, k], Ah_hi[:, t], Ah_lo[:, t],
                                    t == 0, t == T - 1)
                last.then_inc(agg_done, 1)

            def hidden(b, s):
                pe.wait_ge(agg_split, b + 3)
                for f in range(FH):
                    pe.wait_ge(z_stored, b * FH + (f + 1))
                    k = slice(f * P, (f + 1) * P)
                    split_mm(bank[2 + FH * (s % 2) + f][:], W1_hi[:, k], W1_lo[:, k], ag_hi[:, s % 2],
                             ag_lo[:, s % 2], True, True).then_inc(z_done, 1)

            pe.wait_ge(setup_dve, 14)
            pe.wait_ge(Ah_ready, T)
            aggregate(0, 0)
            with pe.Fori(0, B // 2 - 1) as i:
                for s in range(2):
                    aggregate(i * 2 + (s + 1), s + 1)
                    hidden(i * 2 + s, s)
            aggregate(B - 1, 1)
            hidden(B - 2, 0)
            hidden(B - 1, 1)

            pe.wait_ge(Pn_ready, 1)
            pe.wait_ge(agg_split, B + 2)
            pe.wait_ge(z_stored, FH * B + 4)
            for u in range(T):
                for t in range(T):
                    last = pe.transpose(bank[u][:, t * P:(t + 1) * P], Pn_32[:, t, u], ident[:])
                last.then_inc(PT_tr, 1)
            pe.wait_ge(R_ready, 6)
            for j in range(3):
                pe.matmul(bank[4 + j][:, 0:3 * D], raw_f[:], Rp[:, 3 * j:3 * j + 3], start=True,
                          stop=True).then_inc(F_mm, 1)

            def power(src_hi, src_lo, done):
                for u in range(T):
                    for t in range(T):
                        last = split_mm(bank[u][:], Pn_hi[:, t, u], Pn_lo[:, t, u], src_hi[:, t], src_lo[:, t],
                                        t == 0, t == T - 1)
                    last.then_inc(done, 1)

            pe.wait_ge(PT_ready, T)
            power(PT_hi, PT_lo, P2_mm)
            pe.wait_ge(F_evac, 9)
            for j in range(3):
                pe.matmul(bank[4 + j][:, 0:3 * D], b_bc[:], Rp[:, 3 * j:3 * j + 3], start=True,
                          stop=True).then_inc(g_mm, 1)
            pe.wait_ge(g_evac, 9)

            def project(b, s):
                pe.wait_ge(h_split, b + 1)
                pe.wait_ge(o_stored, b + 1)
                for f in range(FH):
                    last = split_mm(bank[6 + s][:], W2_hi[:, f], W2_lo[:, f], h_hi[:, s, f], h_lo[:, s, f],
                                    f == 0, f == FH - 1)
                last.then_inc(o_done, 1)

            with pe.Fori(0, B // 2) as i:
                for s in range(2):
                    project(i * 2 + s, s)

            pe.wait_ge(P2_ready, T)
            power(P2_hi, P2_lo, P3_mm)
            pe.wait_ge(c_link, 3)
            for u in range(T):
                for t in range(T):
                    k = slice(u * P, (u + 1) * P)
                    last = split_mm(bank[4][:, u * P:u * P + 2], PT_hi[:, t, k], PT_lo[:, t, k], c_hi[:, t],
                                    c_lo[:, t], t == 0, t == T - 1)
            last.then_inc(c2_mm, 1)

            def y_nodes(c, s):
                pe.wait_ge(y_ready, c + 1)
                pe.wait_ge(r_ready, c + 1)
                for t in range(T):
                    last = pe.transpose(bank[0][:, t * P:(t + 1) * P], y_T[:, s % 2, t * P:(t + 1) * P], ident[:])
                last.then_inc(y_tr, 1)

            def powers_of_x(c, s):
                pe.wait_ge(x1_ready, c + 1)
                pe.wait_ge(U_split, c * 3 + 1)
                for t in range(T):
                    last = pe.transpose(bank[1][:, t * P:(t + 1) * P], X[:, s % 4, t * D:(t + 1) * D], ident[:])
                last.then_inc(U_done, 1)
                pe.wait_ge(x1_split, c + 1)
                for j, (m_hi, m_lo) in enumerate(((PT_hi, PT_lo), (P2_hi, P2_lo))):
                    pe.wait_ge(U_split, c * 3 + (j + 2))
                    for t in range(T):
                        k = slice(t * D, (t + 1) * D)
                        last = split_mm(bank[2 + j][:], x1_hi[:, s % 2, k], x1_lo[:, s % 2, k], m_hi[:, t],
                                        m_lo[:, t], t == 0, t == T - 1)
                    last.then_inc(U_done, 1)

            def stage_u(c, s, nxt=True):
                if nxt:
                    y_nodes(c + 1, s + 1)
                powers_of_x(c, s)

            def stage_z(c, s):
                pe.wait_ge(U_split, c * 3 + 6)
                for t in range(T):
                    pe.wait_ge(Z_stored, c * T + (t + 1))
                    k = slice(t * P, (t + 1) * P)
                    for j in range(3):
                        last = split_mm(bank[4 + t % 2][:, 0:3 * D], UT_hi[:, s % 2, j, k], UT_lo[:, s % 2, j, k],
                                        G_hi[:, j], G_lo[:, j], j == 0, j == 2)
                    last.then_inc(Z_done, 1)

            def times_p3(hi, lo, g, t, part_ready, need, done):
                for u in range(T):
                    pe.wait_ge(part_ready, need(u))
                    k = slice(t * P, (t + 1) * P)
                    last = split_mm(bank[6 + t % 2][:], P3_hi[:, u, k], P3_lo[:, u, k], hi(u), lo(u), u == 0, u == T - 1)
                last.then_inc(done, 1)

            def stage_v(g):
                for t in range(T):
                    if t >= 2:
                        pe.wait_ge(V_sum, g * T + (t - 1))
                    else:
                        pe.wait_ge(q_ready, g * T + 1)
                    times_p3(lambda u: Z2_hi[:, u], lambda u: Z2_lo[:, u], g, t, Z2_split, lambda u: g * GB + GB,
                             V_done)

            def stage_f(g):
                for t in range(T):
                    if t >= 2:
                        pe.wait_ge(q_ready, g * T + t)
                    else:
                        pe.wait_ge(V_sum, g * T + (t + 3))
                    times_p3(lambda u: V_hi[:, u], lambda u: V_lo[:, u], g, t, V_split, lambda u: g * T + (u + 1),
                             F_done)

            pe.wait_ge(P3_ready, T)
            pe.wait_ge(bn2_ready, 1)
            y_nodes(0, 0)
            pe.wait_ge(G_ready, 1)
            stage_u(0, 0)
            stage_u(1, 1)
            pe.wait_ge(ZB_ready, 1)
            with pe.Fori(0, NG - 1) as g:
                for s in range(GB):
                    stage_z(g * GB + s, s)
                    stage_u(g * GB + (s + 2), s + 2)
                stage_v(g)
                stage_f(g)
            g = NG - 1
            for s in range(GB):
                stage_z(g * GB + s, s)
                if s < 2:
                    stage_u(g * GB + s + 2, s + 2, nxt=s < 1)
            stage_v(g)
            stage_f(g)


_ORDER = ["x", "adj", "L0_gnn_W1", "L0_gnn_b1", "L0_gnn_g1", "L0_gnn_be1", "L0_gnn_W2", "L0_gnn_b2", "L0_gnn_g2",
          "L0_gnn_be2", "L1_gnn_alpha_train", "L1_gnn_w", "L1_gnn_d", "L1_gnn_fc_in_w", "L1_gnn_fc_in_b"]


def kernel(**inputs):
    import numpy as _np
    import concourse.bacc as _bacc
    from concourse import mybir as _mybir
    from concourse.bass_utils import run_bass_kernel_spmd as _run

    nc = _bacc.Bacc("TRN2", target_bir_lowering=False, num_devices=1)
    arrays, args = {}, []
    for name in _ORDER:
        a = _np.ascontiguousarray(inputs[name])
        arrays[f"in_{name}"] = a
        args.append(nc.dram_tensor(f"in_{name}", a.shape, _mybir.dt.from_np(a.dtype), kind="ExternalInput").ap())
    o = nc.dram_tensor("out_0", inputs["x"].shape, F32, kind="ExternalOutput").ap()
    gnn_kernel(nc, *args, o)
    r = _run(nc, [arrays], core_ids=[0])
    return r.results[0]["out_0"]
```

```python
from contextlib import ExitStack
from math import comb

import concourse.bass as bass
from concourse import mybir

F32 = mybir.dt.float32
F32R = mybir.dt.float32r
ALU = mybir.AluOpType
ACT = mybir.ActivationFunctionType
AX = mybir.AxisListType


P = 128
EPS = 1e-5
STEPS = 8
DT = 1.0 / STEPS


def gnn_kernel(nc, x, adj, W1, b1, g1, be1, W2, b2, g2, be2, alpha, w, d, fin_w, fin_b, out):
    B, N, D = x.shape
    H = W1.shape[0]
    T = N // P
    FH = H // P
    GB = 4
    NG = B // GB
    assert D == P and T == 4 and FH == 2 and B % GB == 0 and N == 512

    x_v = x.rearrange("b (p t) d -> b p (t d)", t=T)
    out_v = out.rearrange("b (p t) d -> p b t d", t=T)
    adj_v = adj.rearrange("(p t) m -> p t m", t=T)

    with ExitStack() as ctx:
        base = nc.sbuf_base
        base += -base % 64
        used = {}

        def at(name, kb, shape, dt=F32):
            size = 4
            for n in shape[1:]:
                size *= n
            used[name] = (kb, kb + size / 1024)
            return nc.alloc_sbuf_tensor_at(name, shape, dt, offset=base + int(kb * 1024))

        zT = at("zT", 0, [P, FH, B, N])
        oT = zT[:, 0]
        A2 = at("A2", 0, [P, T, T, P])
        raw_w1 = at("raw_w1", 60, [P, FH, D])
        raw_w2 = at("raw_w2", 61, [P, H])
        raw_w = at("raw_w", 62, [P, D])
        diag_t = at("diag_t", 56, [P, T, P])
        A_sum = at("A_sum", 54, [P, N])
        junk = at("junk", 44, [P, T, N])
        UT_hi = at("UT_hi", 32, [P, 2, 3, N], F32R)
        UT_lo = at("UT_lo", 44, [P, 2, 3, N], F32R)
        x1_hi = at("x1_hi", 56, [P, 2, N], F32R)
        x1_lo = at("x1_lo", 60, [P, 2, N], F32R)
        PT_hi = at("PT_hi", 64, [P, T, N], F32R)
        PT_lo = at("PT_lo", 72, [P, T, N], F32R)
        P2_hi = at("P2_hi", 80, [P, T, N], F32R)
        P2_lo = at("P2_lo", 88, [P, T, N], F32R)
        Ah_hi = at("Ah_hi", 96, [P, T, N], F32R)
        Ah_lo = at("Ah_lo", 104, [P, T, N], F32R)
        P3_hi = at("P3_hi", 96, [P, T, N], F32R)
        P3_lo = at("P3_lo", 104, [P, T, N], F32R)
        Pn_hi = at("Pn_hi", 112, [P, T, T, P], F32R)
        Pn_lo = at("Pn_lo", 120, [P, T, T, P], F32R)
        Z2_hi = at("Z2_hi", 112, [P, T, GB, D], F32R)
        Z2_lo = at("Z2_lo", 120, [P, T, GB, D], F32R)
        X_hi = at("X_hi", 128, [P, 2, N], F32R)
        X_lo = at("X_lo", 132, [P, 2, N], F32R)
        ag_hi = at("ag_hi", 136, [P, 2, N], F32R)
        ag_lo = at("ag_lo", 140, [P, 2, N], F32R)
        A_n = at("A_n", 144, [P, T, N])
        h_hi = at("h_hi", 128, [P, 2, FH, 2, N], F32R)
        h_lo = at("h_lo", 144, [P, 2, FH, 2, N], F32R)
        V_hi = at("V_hi", 128, [P, T, GB * D], F32R)
        V_lo = at("V_lo", 136, [P, T, GB * D], F32R)
        Z01 = at("Z01", 144, [P, T, GB, 2, D])
        Pn_32 = at("Pn_32", 152, [P, T, T, P])
        X = at("X", 160, [P, 4, N])
        Rp = at("Rp", 168, [P, STEPS + 1, D])
        g_row = at("g_row", 172.5, [P, 3, 3 * D])
        G_32 = at("G_32", 177, [P, 3, 3, D])
        zb_tmp = at("zb_tmp", 177, [P, 3 * D])
        Z2 = at("Z2", 201, [P, T, D])
        V_32 = at("V_32", 168, [P, 2, GB * D])
        y_out = at("y_out", 172, [P, T, GB, D])
        G_hi = at("G_hi", 181.5, [P, 3, 3, D], F32R)
        G_lo = at("G_lo", 186, [P, 3, 3, D], F32R)
        ZB = at("ZB", 190.5, [P, T, 3 * D])
        W1_hi = at("W1_hi", 196.5, [P, H], F32R)
        W1_lo = at("W1_lo", 197.5, [P, H], F32R)
        W2_hi = at("W2_hi", 198.5, [P, FH, D], F32R)
        W2_lo = at("W2_lo", 199.5, [P, FH, D], F32R)
        y_T = at("y_T", 196.5, [P, 2, N])
        ident = at("ident", 200.5, [P, P])
        raw_f = at("raw_f", 201, [P, D])
        vec = at("vec", 201.5, [P, P])
        wT = at("wT", 202, [P, D])
        wTd = at("wTd", 202.5, [P, D])
        b_bc = at("b_bc", 203, [P, P])
        g_tmp = at("g_tmp", 203.5, [P, D])
        vecT = at("vecT", 204, [P, 16])
        st1 = at("st1", 204.25, [P, FH, B, 6])
        st2 = at("st2", 205, [P, B, 6])
        c_row = at("c_row", 201, [P, N])
        ones_c = at("ones_c", 205.5, [P, 2])
        small = at("small", 205.625, [P, 64])
        st_x = at("st_x", 206, [P, T, 6])
        st_y = at("st_y", 206.25, [P, GB, 6])
        c_hl = at("c_hl", 206.5, [P, T, 2], F32R)
        small2 = at("small2", 206.625, [P, 32])
        small3 = at("small3", 206.75, [P, 64])
        assert base + 207 * 1024 <= nc.sbuf_usable_end

        B1, G1, BE1, B2, G2, BE2, DV, FB = 0, 2, 4, 6, 7, 8, 9, 10
        col = lambda k, n=T: small[:, k:k + n]
        rs, cs, dg, deg, sd, dinv, al, c_n, c_d, al_in = (col(4 * i) for i in range(10))
        mv1, v1e, rstd1, s1, t1 = col(40, 4), col(44, 2), col(46, 2), col(48, 2), col(50, 2)
        mv2, v2e, rstd2, s2, t2 = col(52, 2), col(54, 1), col(55, 1), col(56, 1), col(57, 1)
        c1, d_cl, eps_t = col(58, 4), col(62, 1), col(63, 1)
        mvx, sdx, rsx, nmx = small2[:, 0:8], small2[:, 8:12], small2[:, 12:16], small2[:, 16:20]
        c2, ms, sq_warm = small2[:, 20:24], small2[:, 24:28], small2[:, 28:29]
        mvy, sdy, rsy, nmy = ([small3[:, 20 * i + a:20 * i + z] for i in range(2)]
                              for a, z in ((0, 8), (8, 12), (12, 16), (16, 20)))

        wide = [ctx.enter_context(nc.psum_tensor(f"banks{2 * i}", [P, 2, 512], F32)) for i in range(4)]
        bank = [wide[i // 2][:, i % 2] for i in range(8)]

        def sem(name):
            return ctx.enter_context(nc.semaphore(name))

        adj_in, vec_in, w_in, w12_in, f_in, alpha_in = (sem(n) for n in (
            "adj_in", "vec_in", "w_in", "w12_in", "f_in", "alpha_in"))
        x_in = [sem(f"x_in{i}") for i in range(4)]
        out_sent = [sem(f"out_sent{t}") for t in range(T)]
        id_zero, id_ready, consts_ready = sem("id_zero"), sem("id_ready"), sem("consts_ready")
        vec_tr, w_tr, w12_tr, vec_ready, wT_ready, W_hi_ready, W_ready = (sem(n) for n in (
            "vec_tr", "w_tr", "w12_tr", "vec_ready", "wT_ready", "W_hi_ready", "W_ready"))
        A_sum_ready, cs_done, rs_ready, deg_link, deg_ready, sd_ready, dinv_ready = (sem(n) for n in (
            "A_sum_ready", "cs_done", "rs_ready", "deg_link", "deg_ready", "sd_ready", "dinv_ready"))
        A2_scaled, A2_ready, Ah_tr, Ah_hi_ready, Ah_ready = (sem(n) for n in (
            "A2_scaled", "A2_ready", "Ah_tr", "Ah_hi_ready", "Ah_ready"))
        al_ready, cn_ready, pool_link, Pn_ready = sem("al_ready"), sem("cn_ready"), sem("pool_link"), sem("Pn_ready")
        R_mm, R_ready = sem("R_mm"), sem("R_ready")
        X_hi_ready, X_split, agg_done, ag_hi_ready, agg_split = (sem(n) for n in (
            "X_hi_ready", "X_split", "agg_done", "ag_hi_ready", "agg_split"))
        z_done, z_stored, bn_link, bn_sq, bn_sd = (sem(n) for n in ("z_done", "z_stored", "bn_link", "bn_sq", "bn_sd"))
        bn1_ready, bn2_ready = sem("bn1_ready"), sem("bn2_ready")
        h_ready, h_hi_ready, h_hi_act, h_split, o_done, o_stored = (sem(n) for n in (
            "h_ready", "h_hi_ready", "h_hi_act", "h_split", "o_done", "o_stored"))
        PT_tr, PT_hi_ready, PT_ready = sem("PT_tr"), sem("PT_hi_ready"), sem("PT_ready")
        P2_mm, P2_hi_ready, P2_ready = sem("P2_mm"), sem("P2_hi_ready"), sem("P2_ready")
        P3_mm, P3_hi_ready, P3_ready = sem("P3_mm"), sem("P3_hi_ready"), sem("P3_ready")
        F_mm, F_evac = sem("F_mm"), sem("F_evac")
        G_hi_ready, G_ready = sem("G_hi_ready"), sem("G_ready")
        c_link, c2_mm, c2_row, c2_ready = sem("c_link"), sem("c2_mm"), sem("c2_row"), sem("c2_ready")
        zb_link, ZB_ready = sem("zb_link"), sem("ZB_ready")
        y_ready, y_tr, r_ready, xs_link, x_mom, x_sd, x_rstd, x_norm, x1_ready, x1_hi_ready, x1_split = (sem(n) for n in (
            "y_ready", "y_tr", "r_ready", "xs_link", "x_mom", "x_sd", "x_rstd", "x_norm", "x1_ready", "x1_hi_ready",
            "x1_split"))
        U_done, U_hi_ready, U_split = sem("U_done"), sem("U_hi_ready"), sem("U_split")
        Z_done, Z_stored, Z2_hi_ready, Z2_split = sem("Z_done"), sem("Z_stored"), sem("Z2_hi_ready"), sem("Z2_split")
        V_done, V_sum, V_hi_ready, V_split = sem("V_done"), sem("V_sum"), sem("V_hi_ready"), sem("V_split")
        F_done, q_ready, ys_link, y_mom, y_sd, y_rstd, y_norm, out_ready = (sem(n) for n in (
            "F_done", "q_ready", "ys_link", "y_mom", "y_sd", "y_rstd", "y_norm", "out_ready"))

        block = ctx.enter_context(nc.Block())

        HEAD = 4
        PAIRS = B // 2
        EXTRA = {(0, "a"): ("R", 2), (0, "h"): ("R", 3), (1, "a"): ("R", 5), (1, "h"): ("F", 0), (2, "a"): ("F", 1),
                 (2, "h"): ("F", 2), (3, "a"): ("F", 3), (3, "h"): ("F", 4), (4, "h"): ("F", 5)}
        PT_bank = lambda u: bank[7 - u % 2]
        extra_bank = lambda key: bank[6 + list(EXTRA).index(key) % 2]

        @block.sync
        def _(sp):
            sp.dma_start(al_in, alpha.rearrange("(p t) -> p t", t=T)).then_inc(alpha_in, 16)
            sp.dma_start(A_n[:], adj_v).then_inc(adj_in, 16)
            for s in range(2):
                sp.dma_start(X[:, s], x_v[s]).then_inc(x_in[s], 16)
            sp.dma_start(raw_w[:], w).then_inc(w_in, 16)
            sp.dma_start(raw_w1[:], W1.rearrange("(f p) d -> p f d", p=P)).then_inc(w12_in, 16)
            sp.dma_start(raw_w2[:], W2).then_inc(w12_in, 16)
            sp.wait_ge(id_zero, 2)
            for row, v in ((B1, b1), (G1, g1), (BE1, be1)):
                sp.dma_start(vec[row:row + FH, :], v.rearrange("(f p) -> f p", p=P)).then_inc(vec_in, 16)
            for row, v in ((B2, b2), (G2, g2), (BE2, be2), (DV, d), (FB, fin_b)):
                sp.dma_start(vec[row:row + 1, :], v.rearrange("(a p) -> a p", a=1)).then_inc(vec_in, 16)
            for s in range(2, 4):
                sp.dma_start(X[:, s], x_v[s]).then_inc(x_in[s], 16)
            sp.dma_start(raw_f[:], fin_w).then_inc(f_in, 16)
            with sp.Fori(1, B // 4) as i:
                for s in range(4):
                    sp.wait_ge(X_split, i * 4 + (s - 3))
                    sp.dma_start(X[:, s], x_v[i * 4 + s]).then_inc(x_in[s], 16)
            for s in range(4):
                sp.wait_ge(X_split, B - 3 + s)
                sp.dma_start(X[:, s], x_v[s]).then_inc(x_in[s], 16)

            def send(g):
                for t in range(T):
                    sp.wait_ge(out_ready, g * T + (t + 1))
                    sp.dma_start(out_v[:, bass.ds(g * GB, GB), t, :], y_out[:, t]).then_inc(out_sent[t], 16)

            with sp.Fori(1, NG) as g:
                for s in range(4):
                    sp.wait_ge(U_done, (g * 4 + (s - 3)) * 3)
                    sp.dma_start(X[:, s], x_v[g * 4 + s]).then_inc(x_in[s], 16)
                send(g - 1)
            send(NG - 1)
            for t in range(T):
                sp.wait_ge(out_sent[t], 16 * (NG + 1))

        @block.gpsimd
        def _(pool):
            pool.memset(ident[:], 0.0).then_inc(id_zero, 1)
            pool.memset(vec[:], 0.0).then_inc(id_zero, 1)
            pool.wait_ge(id_zero, 2)
            pool.affine_select(out=ident[:], in_=ident[:], compare_op=ALU.not_equal, fill=1.0, base=0,
                               pattern=[[-1, P]], channel_multiplier=1).then_inc(id_ready, 1)
            pool.memset(ones_c[:], 1.0)
            pool.memset(eps_t, EPS).then_inc(consts_ready, 1)
            link = 0
            pool.wait_ge(adj_in, 16)
            pool.wait_ge(cn_ready, 2)
            for t in range(T):
                last = pool.tensor_scalar(Pn_32[:, t], A_n[:, t].rearrange("p (q u) -> p u q", u=T),
                                          c_n[:, t:t + 1], 1.0, ALU.mult, ALU.mult)
            last.then_inc(pool_link, 1)
            link += 1
            for t in range(T):
                pool.wait_ge(pool_link, link)
                pool.wait_ge(id_ready, 1)
                pool.tensor_scalar(g_tmp[:], ident[:], c_d[:, t:t + 1], 1.0, ALU.mult, ALU.mult).then_inc(pool_link, 1)
                link += 1
                pool.wait_ge(pool_link, link)
                pool.tensor_tensor(Pn_32[:, t, t], Pn_32[:, t, t], g_tmp[:], ALU.add).then_inc(pool_link, 1)
                link += 1
            pool.wait_ge(pool_link, link)
            pool.tensor_copy(Pn_hi[:], Pn_32[:]).then_inc(pool_link, 1)
            link += 1
            pool.wait_ge(pool_link, link)
            pool.tensor_tensor(Pn_lo[:], Pn_32[:], Pn_hi[:].bitcast(F32), ALU.subtract).then_inc(Pn_ready, 1)
            pool.wait_ge(F_evac, 9)
            for k in range(STEPS):
                for m in range(STEPS - k):
                    coef = DT * comb(m + k, k) + (1.0 if k == 0 and m == 0 else 0.0)
                    src = ident[:] if m == 0 else Rp[:, m]
                    pool.wait_ge(pool_link, link)
                    pool.tensor_scalar(g_tmp[:], src, coef, 1.0, ALU.mult, ALU.mult).then_inc(pool_link, 1)
                    link += 1
                    pool.wait_ge(pool_link, link)
                    dst = G_32[:, k % 3, k // 3]
                    pool.tensor_tensor(dst, dst, g_tmp[:], ALU.add).then_inc(pool_link, 1)
                    link += 1
            pool.wait_ge(pool_link, link)
            pool.tensor_copy(G_hi[:], G_32[:]).then_inc(G_hi_ready, 1)
            pool.wait_ge(G_hi_ready, 1)
            pool.tensor_tensor(G_lo[:], G_32[:], G_hi[:].bitcast(F32), ALU.subtract).then_inc(G_ready, 1)
            pool.wait_ge(F_evac, 18)
            pool.wait_ge(c_link, 2)
            pool.wait_ge(G_ready, 1)
            zb = 0
            for c, k in ((c1, 1), (c2, 2)):
                if k == 2:
                    pool.wait_ge(c2_ready, 1)
                for t in range(T):
                    if zb:
                        pool.wait_ge(zb_link, zb)
                    pool.tensor_scalar(zb_tmp[:], g_row[:, k], c[:, t:t + 1], 1.0, ALU.mult, ALU.mult).then_inc(zb_link, 1)
                    pool.wait_ge(zb_link, zb + 1)
                    zb += 2
                    pool.tensor_tensor(ZB[:, t], g_row[:, 0] if k == 1 else ZB[:, t], zb_tmp[:],
                                       ALU.add).then_inc(zb_link if zb < 4 * T else ZB_ready, 1)

        @block.scalar
        def _(act):
            act.wait_ge(alpha_in, 16)
            act.activation(al, al_in, ACT.Sigmoid).then_inc(al_ready, 1)
            act.wait_ge(consts_ready, 1)
            act.activation(sq_warm, eps_t, ACT.Sqrt)
            act.wait_ge(adj_in, 16)
            for t in range(T):
                last = act.activation(junk[:, t], A_n[:, t], ACT.Copy, accum_out=rs[:, t:t + 1])
            last.then_inc(rs_ready, 1)
            act.wait_ge(deg_ready, 1)
            act.activation(sd, deg, ACT.Sqrt).then_inc(sd_ready, 1)
            act.wait_ge(dinv_ready, 1)
            for t in (1, 3):
                act.activation(A2[:, t], A_n[:, t].rearrange("p (q u) -> p u q", u=T), ACT.Copy,
                               scale=dinv[:, t:t + 1]).then_inc(A2_scaled, 1)
            for b in range(2):
                act.wait_ge(x_in[b], 16)
                act.activation(X_hi[:, b], X[:, b], ACT.Copy).then_inc(X_hi_ready, 1)
            for t in range(T):
                act.wait_ge(Ah_tr, t + 1)
                act.activation(Ah_hi[:, t], bank[t], ACT.Copy, scale=dinv[:, t:t + 1]).then_inc(Ah_hi_ready, 1)
            act.wait_ge(w12_tr, 1)
            act.activation(W1_hi[:], bank[5][:, 0:H], ACT.Copy)
            act.activation(W2_hi[:].rearrange("p f d -> p (f d)"), bank[5][:, H:2 * H], ACT.Copy).then_inc(W_hi_ready, 1)
            act.sem_inc(z_stored, 4)
            act.wait_ge(vec_ready, 1)

            def extra(key):
                kind, j = EXTRA.get(key, ("", 0))
                if kind != "F":
                    return
                act.wait_ge(F_mm, j + 1)
                for m in range(3 * (j % 3), 3 * (j % 3) + 3):
                    k = STEPS - m
                    dst = G_32[:, k % 3, k // 3] if j < 3 else g_row[:, k % 3, (k // 3) * D:(k // 3 + 1) * D]
                    act.activation(dst, extra_bank(key)[:, (m % 3) * D:(m % 3 + 1) * D], ACT.Copy,
                                   scale=float(comb(STEPS, k))).then_inc(F_evac, 1)

            def layer1(b, s, x_wait, more=True, head=False):
                act.wait_ge(agg_done, b + 1)
                act.activation(ag_hi[:, s % 2], bank[s % 2], ACT.Copy).then_inc(ag_hi_ready, 1)
                if more:
                    act.wait_ge(x_in[(s + 2) % 4], x_wait)
                    act.activation(X_hi[:, s % 2], X[:, (s + 2) % 4], ACT.Copy).then_inc(X_hi_ready, 1)
                if head:
                    extra((b, "a"))
                for f in range(FH):
                    act.wait_ge(z_done, b * FH + (f + 1))
                    act.activation(zT[:, f, b, :], bank[2 + FH * (s % 2) + f], ACT.Identity,
                                   bias=vecT[:, B1 + f:B1 + f + 1]).then_inc(z_stored, 1)
                if head:
                    extra((b, "h"))

            for s in range(HEAD):
                layer1(s, s, (1 + (s + 2) // 4) * 16, head=True)
            with act.Fori(1, B // 4 - 1) as i:
                for s in range(4):
                    layer1(i * 4 + s, s, (i + 1 + (s + 2) // 4) * 16)
            for s in range(4):
                layer1(B - 4 + s, s, B // 4 * 16, more=s < 2)
                if s == 0:
                    extra((HEAD, "h"))
                act.wait_ge(PT_tr, s + 1)
                act.activation(PT_hi[:, s], PT_bank(s), ACT.Copy).then_inc(PT_hi_ready, 1)
            act.wait_ge(bn_sq, 1)
            act.activation(v1e, mv1.rearrange("p (f two) -> p f two", two=2)[:, :, 1], ACT.Sqrt,
                           bias=eps_t).then_inc(bn_sd, 1)

            def relu(j, s):
                for f in (1, 0):
                    z = zT[:, f, bass.ds(j * 2, 2), :]
                    act.activation(z, z, ACT.Relu, bias=t1[:, f:f + 1], scale=s1[:, f:f + 1]).then_inc(h_ready, 1)

            def h_high(j, s):
                act.wait_ge(h_ready, j * 2 + 1)
                act.activation(h_hi[:, s, 1, 1], zT[:, 1, j * 2 + 1, :], ACT.Copy).then_inc(h_hi_act, 1)

            def store_o(j, s):
                act.wait_ge(o_done, j + 1)
                act.activation(oT[:, bass.ds(j * 2, 2), :], wide[2 + s][:], ACT.Identity,
                               bias=vecT[:, B2:B2 + 1]).then_inc(o_stored, 1)

            act.wait_ge(bn1_ready, 1)
            act.sem_inc(o_stored, 2)
            for s in range(2):
                relu(s, s)
                h_high(s, s)
            for t in range(T):
                act.wait_ge(P2_mm, t + 1)
                act.activation(P2_hi[:, t], bank[t], ACT.Copy).then_inc(P2_hi_ready, 1)

            def p3_high(t):
                act.wait_ge(P3_mm, t + 1)
                act.activation(P3_hi[:, t], bank[t], ACT.Copy).then_inc(P3_hi_ready, 1)

            with act.Fori(0, PAIRS // 2 - 1) as i:
                for s in range(2):
                    relu(i * 2 + (s + 2), s)
                    store_o(i * 2 + s, s)
                    h_high(i * 2 + (s + 2), s)
            store_o(PAIRS - 2, 0)
            p3_high(0)
            p3_high(1)
            store_o(PAIRS - 1, 1)

            act.wait_ge(bn_sq, 2)
            act.activation(v2e, mv2[:, 1:2], ACT.Sqrt, bias=eps_t).then_inc(bn_sd, 1)
            act.wait_ge(bn2_ready, 1)

            def affine(c, s):
                act.activation(y_T[:, s % 2], oT[:, c, :], ACT.Identity, bias=t2, scale=s2).then_inc(y_ready, 1)

            def root(c):
                act.wait_ge(x_mom, c + 1)
                act.activation(sdx, mvx.rearrange("p (t two) -> p t two", two=2)[:, :, 1], ACT.Sqrt,
                               bias=eps_t).then_inc(x_sd, 1)

            def normalize(c, s):
                act.wait_ge(x_norm, c + 1)
                for t in range(T):
                    part = X[:, s % 4, t * D:(t + 1) * D]
                    last = act.activation(part, part, ACT.Identity, bias=nmx[:, t:t + 1], scale=rsx[:, t:t + 1])
                last.then_inc(x1_ready, 1)

            def x1_high(c, s):
                act.wait_ge(x1_ready, c + 1)
                act.activation(x1_hi[:, s % 2], X[:, s % 4], ACT.Copy).then_inc(x1_hi_ready, 1)

            def u_high(c, s, j):
                act.wait_ge(U_done, c * 3 + (j + 1))
                act.activation(UT_hi[:, s % 2, j], bank[1 + j], ACT.Copy).then_inc(U_hi_ready, 1)

            def stage_u(c, s, nxt=True, nxt2=True):
                u_high(c, s, 0)
                if nxt2:
                    affine(c + 2, s)
                if nxt:
                    root(c + 1)
                u_high(c, s, 1)
                if nxt:
                    normalize(c + 1, s + 1)
                u_high(c, s, 2)
                if nxt:
                    x1_high(c + 1, s + 1)

            def stage_z(c, s):
                act.wait_ge(Z_stored, c * T + (T + 2))
                act.activation(Z2_hi[:, :, s % GB, :], Z2[:], ACT.Copy).then_inc(Z2_hi_ready, 1)

            def stage_v(g):
                for t in range(T):
                    act.wait_ge(V_sum, g * T + (t + 1))
                    act.activation(V_hi[:, t], V_32[:, t % 2], ACT.Copy).then_inc(V_hi_ready, 1)

            def out_root(g, t):
                act.wait_ge(y_mom, g * T + (t + 1))
                act.activation(sdy[t % 2], mvy[t % 2].rearrange("p (t two) -> p t two", two=2)[:, :, 1], ACT.Sqrt,
                               bias=eps_t).then_inc(y_sd, 1)

            def out_normalize(g, t):
                act.wait_ge(y_norm, g * T + (t + 1))
                for s in range(GB):
                    part = y_out[:, t, s]
                    last = act.activation(part, part, ACT.Identity, bias=nmy[t % 2][:, s:s + 1],
                                          scale=rsy[t % 2][:, s:s + 1])
                last.then_inc(out_ready, 1)

            def stage_f(g):
                for t in range(T):
                    out_root(g, t)
                    if t:
                        out_normalize(g, t - 1)
                out_normalize(g, T - 1)

            affine(0, 0)
            affine(1, 1)
            p3_high(2)
            root(0)
            normalize(0, 0)
            x1_high(0, 0)
            p3_high(3)
            stage_u(0, 0)
            stage_u(1, 1)
            with act.Fori(0, NG - 1) as g:
                for s in range(GB):
                    stage_z(g * GB + s, s)
                    stage_u(g * GB + (s + 2), s + 2)
                stage_v(g)
                stage_f(g)
            g = NG - 1
            for s in range(GB):
                stage_z(g * GB + s, s)
                if s < 2:
                    stage_u(g * GB + s + 2, s + 2, nxt=s < 1, nxt2=False)
            stage_v(g)
            stage_f(g)

        @block.vector
        def _(dve):
            dve.wait_ge(adj_in, 16)
            dve.reduce_sum(A_sum[:], A_n[:].rearrange("p t m -> p m t"), AX.X).then_inc(A_sum_ready, 1)
            dve.wait_ge(id_ready, 1)
            for t in range(T):
                last = dve.tensor_tensor(diag_t[:, t], A_n[:, t].rearrange("p (q u) -> p u q", u=T)[:, t], ident[:],
                                         ALU.mult)
            last.then_inc(deg_link, 1)
            dve.wait_ge(deg_link, 1)
            dve.reduce_sum(dg, diag_t[:], AX.X).then_inc(deg_link, 1)
            dve.wait_ge(rs_ready, 1)
            dve.wait_ge(deg_link, 2)
            dve.tensor_tensor(cs, rs, dg, ALU.subtract).then_inc(deg_link, 1)
            dve.wait_ge(al_ready, 1)
            dve.tensor_scalar(c_n, al, DT * 0.5, None, ALU.mult).then_inc(cn_ready, 1)
            dve.tensor_scalar(c_d, al, -DT * 0.5, 1.0 - DT, ALU.mult, ALU.add).then_inc(cn_ready, 1)
            dve.wait_ge(cs_done, 1)
            dve.wait_ge(deg_link, 3)
            dve.scalar_tensor_tensor(out=deg, in0=bank[4][:, 0:T], scalar=1.0, in1=cs, op0=ALU.add,
                                     op1=ALU.add).then_inc(deg_ready, 1)
            dve.wait_ge(sd_ready, 1)
            dve.reciprocal(dinv, sd).then_inc(dinv_ready, 1)
            dve.wait_ge(dinv_ready, 1)
            for t in (0, 2):
                dve.tensor_scalar(A2[:, t], A_n[:, t].rearrange("p (q u) -> p u q", u=T), dinv[:, t:t + 1],
                                  None, ALU.mult).then_inc(A2_scaled, 1)
            dve.wait_ge(A2_scaled, 4)
            for t in range(T):
                dve.scalar_tensor_tensor(out=A2[:, t, t], in0=ident[:], scalar=dinv[:, t:t + 1],
                                         in1=A2[:, t, t], op0=ALU.mult, op1=ALU.add).then_inc(A2_ready, 1)
            dve.wait_ge(vec_tr, 1)
            dve.tensor_copy(vecT[:], bank[6][:, 0:16]).then_inc(vec_ready, 1)
            dve.wait_ge(vec_ready, 1)
            dve.tensor_scalar(d_cl, vecT[:, DV:DV + 1], 0.0, 1.0, ALU.max, ALU.min)
            dve.wait_ge(w_tr, 1)
            dve.tensor_copy(wT[:], bank[7][:, 0:D]).then_inc(wT_ready, 1)
            dve.wait_ge(wT_ready, 1)
            dve.tensor_scalar(wTd[:], wT[:], d_cl, None, ALU.mult).then_inc(wT_ready, 1)
            for b in range(2):
                dve.wait_ge(X_hi_ready, b + 1)
                dve.tensor_tensor(X_lo[:, b], X[:, b], X_hi[:, b].bitcast(F32), ALU.subtract).then_inc(X_split, 1)
            dve.wait_ge(cn_ready, 2)
            for t in range(T):
                last = dve.scalar_tensor_tensor(out=c1[:, t:t + 1], in0=rs[:, t:t + 1], scalar=c_n[:, t:t + 1],
                                                in1=c_d[:, t:t + 1], op0=ALU.mult, op1=ALU.add)
            last.then_inc(c_link, 1)
            dve.wait_ge(c_link, 1)
            dve.tensor_copy(c_hl[:, :, 0], c1).then_inc(c_link, 1)
            dve.wait_ge(c_link, 2)
            dve.tensor_tensor(c_hl[:, :, 1], c1, c_hl[:, :, 0].bitcast(F32), ALU.subtract).then_inc(c_link, 1)
            for t in range(T):
                dve.wait_ge(Ah_hi_ready, t + 1)
                dve.scalar_tensor_tensor(out=Ah_lo[:, t], in0=bank[t], scalar=dinv[:, t:t + 1],
                                         in1=Ah_hi[:, t].bitcast(F32), op0=ALU.mult,
                                         op1=ALU.subtract).then_inc(Ah_ready, 1)
            dve.wait_ge(W_hi_ready, 1)
            dve.tensor_tensor(W1_lo[:], bank[5][:, 0:H], W1_hi[:].bitcast(F32), ALU.subtract).then_inc(W_ready, 1)
            dve.tensor_tensor(W2_lo[:].rearrange("p f d -> p (f d)"), bank[5][:, H:2 * H],
                              W2_hi[:].rearrange("p f d -> p (f d)").bitcast(F32), ALU.subtract).then_inc(W_ready, 1)
            dve.wait_ge(R_mm, 1)
            dve.tensor_scalar(Rp[:, 1], bank[7][:, 0:D], DT, None, ALU.mult).then_inc(R_ready, 1)
            dve.tensor_scalar(Rp[:, 0], ident[:], 1.0, None, ALU.mult).then_inc(R_ready, 1)
            dve.tensor_scalar(b_bc[:], ident[:], 0.0, vecT[:, FB:FB + 1], ALU.mult, ALU.add).then_inc(R_ready, 1)

            dve.sem_inc(agg_split, 2)
            powers = {2: (2, 3, 2), 3: (3, 5, 3), 5: (5, 9, 4)}

            def extra(key):
                kind, j = EXTRA.get(key, ("", 0))
                if kind == "R":
                    a, z, n = powers[j]
                    dve.wait_ge(R_mm, n)
                    dve.tensor_copy(Rp[:, a:z].rearrange("p m d -> p (m d)"),
                                    extra_bank(key)[:, 0:(z - a) * D]).then_inc(R_ready, 1)

            def layer1(b, s, more=True, head=False):
                dve.wait_ge(ag_hi_ready, b + 1)
                dve.tensor_tensor(ag_lo[:, s % 2], bank[s % 2], ag_hi[:, s % 2].bitcast(F32),
                                  ALU.subtract).then_inc(agg_split, 1)
                if more:
                    dve.wait_ge(X_hi_ready, b + 3)
                    dve.tensor_tensor(X_lo[:, s % 2], X[:, (s + 2) % 4], X_hi[:, s % 2].bitcast(F32),
                                      ALU.subtract).then_inc(X_split, 1)
                if head:
                    extra((b, "a"))
                for f in range(FH):
                    dve.wait_ge(z_stored, b * FH + (f + 1 + 4))
                    last = dve.bn_stats(st1[:, f, b, :], zT[:, f, b, :])
                if not more:
                    last.then_inc(bn_link, 1)
                if head:
                    extra((b, "h"))

            for s in range(HEAD):
                layer1(s, s, head=True)
            with dve.Fori(1, B // 4 - 1) as i:
                for s in range(4):
                    layer1(i * 4 + s, s)
            def pt_low(t):
                dve.wait_ge(PT_hi_ready, t + 1)
                dve.tensor_tensor(PT_lo[:, t], PT_bank(t), PT_hi[:, t].bitcast(F32), ALU.subtract).then_inc(PT_ready, 1)

            for s in range(4):
                if s:
                    pt_low(s - 1)
                layer1(B - 4 + s, s, more=s < 2)

            dve.wait_ge(bn_link, 2)
            for f in range(FH):
                last = dve.bn_aggr(mv1[:, 2 * f:2 * f + 2], st1[:, f].rearrange("p b k -> p (b k)"))
            last.then_inc(bn_sq, 1)
            pt_low(T - 1)
            dve.wait_ge(bn_sd, 1)
            dve.reciprocal(rstd1, v1e).then_inc(bn_link, 1)
            dve.wait_ge(bn_link, 3)
            dve.tensor_tensor(s1, rstd1, vecT[:, G1:G1 + FH], ALU.mult).then_inc(bn_link, 1)
            dve.wait_ge(bn_link, 4)
            dve.tensor_tensor(ms[:, 0:FH], mv1.rearrange("p (f two) -> p f two", two=2)[:, :, 0], s1,
                              ALU.mult).then_inc(bn_link, 1)
            dve.wait_ge(bn_link, 5)
            dve.tensor_tensor(t1, vecT[:, BE1:BE1 + FH], ms[:, 0:FH], ALU.subtract).then_inc(bn1_ready, 1)
            def split_h(j, s, o_wait=None):
                if o_wait is not None:
                    dve.wait_ge(o_done, o_wait)
                dve.wait_ge(h_ready, j * 2 + 1)
                dve.tensor_copy(h_hi[:, s, 1, 0], zT[:, 1, j * 2, :])
                dve.wait_ge(h_ready, j * 2 + 2)
                dve.tensor_copy(h_hi[:, s, 0], zT[:, 0, bass.ds(j * 2, 2), :]).then_inc(h_hi_ready, 1)
                dve.wait_ge(h_hi_ready, j + 1)
                dve.wait_ge(h_hi_act, j + 1)
                for f in range(FH):
                    last = dve.tensor_tensor(h_lo[:, s, f], zT[:, f, bass.ds(j * 2, 2), :],
                                             h_hi[:, s, f].bitcast(F32), ALU.subtract)
                last.then_inc(h_split, 1)

            def stats_o(j, s, end=False):
                dve.wait_ge(o_stored, j + 3)
                for e in range(2):
                    last = dve.bn_stats(st2[:, j * 2 + e, :], oT[:, j * 2 + e, :])
                if end:
                    last.then_inc(bn_link, 1)

            split_h(0, 0)
            dve.wait_ge(c2_mm, 1)
            dve.tensor_copy(c_row[0:2], bank[6][0:2]).then_inc(c2_row, 1)
            split_h(1, 1)
            dve.wait_ge(c2_mm, 2)
            dve.tensor_copy(c2, bank[7][:, 0:T]).then_inc(c2_ready, 1)
            for t in range(T):
                dve.wait_ge(P2_hi_ready, t + 1)
                dve.tensor_tensor(P2_lo[:, t], bank[t], P2_hi[:, t].bitcast(F32), ALU.subtract).then_inc(P2_ready, 1)

            def p3_low(t):
                dve.wait_ge(P3_hi_ready, t + 1)
                dve.tensor_tensor(P3_lo[:, t], bank[t], P3_hi[:, t].bitcast(F32), ALU.subtract).then_inc(P3_ready, 1)

            with dve.Fori(0, PAIRS // 2 - 1) as i:
                for s in range(2):
                    split_h(i * 2 + (s + 2), s, i * 2 + (s + 1))
                    stats_o(i * 2 + s, s)
            stats_o(PAIRS - 2, 0)
            p3_low(0)
            p3_low(1)
            stats_o(PAIRS - 1, 1, end=True)
            dve.wait_ge(bn_link, 6)
            dve.bn_aggr(mv2, st2[:].rearrange("p b k -> p (b k)")).then_inc(bn_sq, 1)
            dve.wait_ge(bn_sd, 2)
            dve.reciprocal(rstd2, v2e).then_inc(bn_link, 1)
            dve.wait_ge(bn_link, 7)
            dve.tensor_tensor(s2, rstd2, vecT[:, G2:G2 + 1], ALU.mult).then_inc(bn_link, 1)
            dve.wait_ge(bn_link, 8)
            dve.tensor_tensor(ms[:, 2:3], mv2[:, 0:1], s2, ALU.mult).then_inc(bn_link, 1)
            dve.wait_ge(bn_link, 9)
            dve.tensor_tensor(t2, vecT[:, BE2:BE2 + 1], ms[:, 2:3], ALU.subtract).then_inc(bn2_ready, 1)
            dve.sem_inc(r_ready, 1)
            dve.sem_inc(U_split, 3)
            dve.sem_inc(Z_stored, 2)
            dve.sem_inc(q_ready, 1)
            for t in range(T):
                dve.sem_inc(out_sent[t], 16)

            def moments(c, s, x_wait):
                dve.wait_ge(x_in[s % 4], x_wait)
                dve.wait_ge(y_tr, c + 1)
                dve.tensor_tensor(X[:, s % 4], X[:, s % 4], bank[0], ALU.add).then_inc(r_ready, 1)
                dve.wait_ge(r_ready, c + 2)
                for t in range(T):
                    last = dve.bn_stats(st_x[:, t], X[:, s % 4, t * D:(t + 1) * D])
                last.then_inc(xs_link, 1)
                dve.wait_ge(xs_link, c + 1)
                dve.nop(nofuse=True)
                for t in range(T):
                    last = dve.bn_aggr(mvx[:, 2 * t:2 * t + 2], st_x[:, t])
                last.then_inc(x_mom, 1)

            def norm_scale(c):
                dve.wait_ge(x_sd, c + 1)
                dve.reciprocal(rsx, sdx).then_inc(x_rstd, 1)
                dve.wait_ge(x_rstd, c + 1)
                dve.scalar_tensor_tensor(out=nmx, in0=mvx.rearrange("p (t two) -> p t two", two=2)[:, :, 0],
                                         scalar=-1.0, in1=rsx, op0=ALU.mult, op1=ALU.mult).then_inc(x_norm, 1)

            def x1_low(c, s):
                dve.wait_ge(x1_hi_ready, c + 1)
                dve.tensor_tensor(x1_lo[:, s % 2], X[:, s % 4], x1_hi[:, s % 2].bitcast(F32),
                                  ALU.subtract).then_inc(x1_split, 1)

            def u_low(c, s, j):
                dve.wait_ge(U_hi_ready, c * 3 + (j + 1))
                dve.tensor_tensor(UT_lo[:, s % 2, j], bank[1 + j], UT_hi[:, s % 2, j].bitcast(F32),
                                  ALU.subtract).then_inc(U_split, 1)

            def stage_u(c, s, x_wait=None, carry=False):
                u_low(c, s, 0)
                if x_wait is not None:
                    moments(c + 1, s + 1, x_wait)
                    norm_scale(c + 1)
                u_low(c, s, 1)
                if not carry:
                    u_low(c, s, 2)
                    if x_wait is not None:
                        x1_low(c + 1, s + 1)

            def stage_z(c, s, rest=(False, False)):
                for t in range(T):
                    if t == 1 and rest[0]:
                        u_low(c + 1, s + 1, 2)
                    if t == 2 and rest[1]:
                        x1_low(c + 2, s + 2)
                    dve.wait_ge(Z_done, c * T + (t + 1))
                    dve.tensor_tensor(Z01[:, t, s % GB].rearrange("p a d -> p (a d)"), bank[4 + t % 2][:, 0:2 * D],
                                      ZB[:, t, 0:2 * D], ALU.add)
                    dve.tensor_tensor(Z2[:, t], bank[4 + t % 2][:, 2 * D:3 * D], ZB[:, t, 2 * D:3 * D],
                                      ALU.add).then_inc(Z_stored, 1)
                dve.wait_ge(Z2_hi_ready, c + 1)
                dve.tensor_tensor(Z2_lo[:, :, s % GB, :], Z2[:], Z2_hi[:, :, s % GB, :].bitcast(F32),
                                  ALU.subtract).then_inc(Z2_split, 1)

            def flush(c, s):
                u_low(c + 1, s + 1, 2)
                x1_low(c + 2, s + 2)

            def v_low(g, t):
                dve.wait_ge(V_hi_ready, g * T + (t + 1))
                dve.tensor_tensor(V_lo[:, t], V_32[:, t % 2], V_hi[:, t].bitcast(F32),
                                  ALU.subtract).then_inc(V_split, 1)

            def stage_v(g):
                for t in range(T):
                    if t >= 2:
                        dve.wait_ge(V_split, g * T + (t - 1))
                    dve.wait_ge(V_done, g * T + (t + 1))
                    dve.tensor_tensor(V_32[:, t % 2].rearrange("p (s d) -> p s d", d=D),
                                      bank[6 + t % 2].rearrange("p (s d) -> p s d", d=D), Z01[:, t, :, 1],
                                      ALU.add).then_inc(V_sum, 1)
                    if t:
                        v_low(g, t - 1)
                v_low(g, T - 1)

            def out_scale(g, t):
                dve.wait_ge(y_sd, g * T + (t + 1))
                dve.reciprocal(rsy[t % 2], sdy[t % 2]).then_inc(y_rstd, 1)
                dve.wait_ge(y_rstd, g * T + (t + 1))
                dve.scalar_tensor_tensor(out=nmy[t % 2], in0=mvy[t % 2].rearrange("p (t two) -> p t two", two=2)[:, :, 0],
                                         scalar=-1.0, in1=rsy[t % 2], op0=ALU.mult, op1=ALU.mult).then_inc(y_norm, 1)

            def stage_f(g):
                for t in range(T):
                    dve.wait_ge(F_done, g * T + (t + 1))
                    dve.wait_ge(out_sent[t], (g + 1) * 16)
                    dve.tensor_tensor(y_out[:, t], bank[6 + t % 2].rearrange("p (s d) -> p s d", d=D),
                                      Z01[:, t, :, 0], ALU.add).then_inc(q_ready, 1)
                    dve.wait_ge(q_ready, g * T + (t + 2))
                    for s in range(GB):
                        last = dve.bn_stats(st_y[:, s], y_out[:, t, s])
                    last.then_inc(ys_link, 1)
                    dve.wait_ge(ys_link, g * T + (t + 1))
                    dve.nop(nofuse=True)
                    for s in range(GB):
                        last = dve.bn_aggr(mvy[t % 2][:, 2 * s:2 * s + 2], st_y[:, s])
                    last.then_inc(y_mom, 1)
                    if t:
                        out_scale(g, t - 1)
                out_scale(g, T - 1)

            x2 = B // 4
            moments(0, 0, (x2 + 1) * 16)
            p3_low(2)
            norm_scale(0)
            p3_low(3)
            x1_low(0, 0)
            stage_u(0, 0, (x2 + 1) * 16)
            stage_u(1, 1, (x2 + 1) * 16)
            dve.wait_ge(ZB_ready, 1)
            with dve.Fori(0, NG - 1) as g:
                for s in range(GB):
                    stage_z(g * GB + s, s, (s > 0, s > 0))
                    stage_u(g * GB + (s + 2), s + 2, (g + (x2 + 1 + (s + 3) // 4)) * 16, carry=True)
                flush(g * GB + GB, GB)
                stage_v(g)
                stage_f(g)
            g = NG - 1
            for s in range(GB):
                if s:
                    dve.wait_ge(Z2_split, g * GB + s)
                stage_z(g * GB + s, s, (s in (1, 2), s == 1))
                if s < 2:
                    stage_u(g * GB + s + 2, s + 2, (x2 + NG) * 16 if s < 1 else None, carry=True)
            stage_v(g)
            stage_f(g)

        @block.tensor
        def _(pe):
            def split_mm(dst, w_hi, w_lo, m_hi, m_lo, first, last):
                pe.matmul(dst, w_hi, m_hi, start=first, stop=False)
                pe.matmul(dst, w_hi, m_lo, start=False, stop=False)
                return pe.matmul(dst, w_lo, m_hi, start=False, stop=last)

            pe.wait_ge(A_sum_ready, 1)
            pe.wait_ge(consts_ready, 1)
            for u in range(T):
                last = pe.matmul(bank[4][:, u:u + 1], A_sum[:].rearrange("p (q u) -> p u q", u=T)[:, u],
                                 ones_c[:, 0:1], start=True, stop=True)
            last.then_inc(cs_done, 1)
            pe.wait_ge(id_ready, 1)
            pe.wait_ge(vec_in, 8 * 16)
            pe.transpose(bank[6][:, 0:P], vec[:], ident[:]).then_inc(vec_tr, 1)
            pe.wait_ge(w_in, 16)
            pe.transpose(bank[7][:, 0:P], raw_w[:], ident[:]).then_inc(w_tr, 1)
            pe.wait_ge(w12_in, 2 * 16)
            for f in range(FH):
                pe.transpose(bank[5][:, f * P:(f + 1) * P], raw_w1[:, f], ident[:])
            for f in range(FH):
                last = pe.transpose(bank[5][:, H + f * P:H + (f + 1) * P], raw_w2[:, f * P:(f + 1) * P], ident[:])
            last.then_inc(w12_tr, 1)
            for t in range(T):
                pe.wait_ge(A2_ready, t + 1)
                for u in range(T):
                    last = pe.transpose(bank[u][:, t * P:(t + 1) * P], A2[:, t, u], ident[:])
                    if t == T - 1:
                        last.then_inc(Ah_tr, 1)
            pe.wait_ge(wT_ready, 2)
            pe.matmul(bank[7][:, 0:D], wTd[:], wT[:], start=True, stop=True).then_inc(R_mm, 1)

            def aggregate(b, s, first=False):
                pe.wait_ge(X_split, b + 1)
                pe.wait_ge(agg_split, b + 1)
                for t in range(T):
                    if first:
                        pe.wait_ge(Ah_ready, t + 1)
                    k = slice(t * D, (t + 1) * D)
                    last = split_mm(bank[s % 2], X_hi[:, s % 2, k], X_lo[:, s % 2, k], Ah_hi[:, t], Ah_lo[:, t],
                                    t == 0, t == T - 1)
                last.then_inc(agg_done, 1)

            def hidden(b, s):
                pe.wait_ge(agg_split, b + 3)
                for f in range(FH):
                    pe.wait_ge(z_stored, b * FH + (f + 1))
                    k = slice(f * P, (f + 1) * P)
                    split_mm(bank[2 + FH * (s % 2) + f], W1_hi[:, k], W1_lo[:, k], ag_hi[:, s % 2],
                             ag_lo[:, s % 2], True, True).then_inc(z_done, 1)

            def extra(key):
                if key not in EXTRA:
                    return
                kind, j = EXTRA[key]
                dst = extra_bank(key)
                if kind == "R":
                    a, lhs, need = {2: (1, 1, 1), 3: (1, 2, 4), 5: (1, 4, 5)}[j]
                    z = {2: 2, 3: 3, 5: 5}[j]
                    pe.wait_ge(R_ready, need)
                    pe.matmul(dst[:, 0:(z - a) * D], Rp[:, lhs], Rp[:, a:z].rearrange("p m d -> p (m d)"),
                              start=True, stop=True).then_inc(R_mm, 1)
                else:
                    pe.wait_ge(R_ready, 6)
                    pe.wait_ge(f_in, 16)
                    if j >= 2:
                        pe.wait_ge(F_evac, 3 * (j - 1))
                    m = 3 * (j % 3)
                    pe.matmul(dst[:, 0:3 * D], raw_f[:] if j < 3 else b_bc[:],
                              Rp[:, m:m + 3].rearrange("p m d -> p (m d)"), start=True, stop=True).then_inc(F_mm, 1)

            aggregate(0, 0, first=True)
            pe.wait_ge(W_ready, 2)
            for s in range(HEAD):
                aggregate(s + 1, s + 1)
                extra((s, "a"))
                hidden(s, s)
                extra((s, "h"))
            def p_transposed(u):
                for t in range(T):
                    last = pe.transpose(PT_bank(u)[:, t * P:(t + 1) * P], Pn_32[:, t, u], ident[:])
                last.then_inc(PT_tr, 1)

            with pe.Fori(HEAD // 2, B // 2 - 2) as i:
                for s in range(2):
                    aggregate(i * 2 + (s + 1), s + 1)
                    hidden(i * 2 + s, s)
            pe.wait_ge(Pn_ready, 1)
            for s in range(4):
                if s < 3:
                    aggregate(B - 3 + s, s + 1)
                else:
                    pe.wait_ge(PT_ready, 2)
                    p_transposed(3)
                hidden(B - 4 + s, s)
                if s == 0:
                    extra((HEAD, "h"))
                    pe.wait_ge(F_evac, 15)
                    p_transposed(0)
                elif s == 1:
                    pe.wait_ge(F_evac, 18)
                    p_transposed(1)
                elif s == 2:
                    pe.wait_ge(PT_ready, 1)
                    p_transposed(2)

            def power(dst, u, parts, src_hi, src_lo):
                for t in parts:
                    last = split_mm(dst, Pn_hi[:, t, u], Pn_lo[:, t, u], src_hi[:, t], src_lo[:, t],
                                    t == 0, t == T - 1)
                return last

            pe.wait_ge(PT_ready, T)
            pe.wait_ge(agg_split, B + 2)
            for u in range(T):
                if u == 2:
                    pe.wait_ge(z_stored, FH * (B - 1) + 4)
                power(bank[u], u, range(T), PT_hi, PT_lo).then_inc(P2_mm, 1)
            pe.wait_ge(c_link, 3)
            for t in range(T):
                pe.matmul(bank[6][0:2], c_hl[:, t], PT_hi[:, t], start=t == 0, stop=False)
                last = pe.matmul(bank[6][0:2], c_hl[:, t], PT_lo[:, t], start=False, stop=t == T - 1)
            last.then_inc(c2_mm, 1)

            def project(j, s):
                pe.wait_ge(h_split, j + 1)
                pe.wait_ge(o_stored, j + 1)
                for e in range(2):
                    for f in range(FH):
                        last = split_mm(wide[2 + s][:, e], W2_hi[:, f], W2_lo[:, f], h_hi[:, s, f, e],
                                        h_lo[:, s, f, e], f == 0, f == FH - 1)
                last.then_inc(o_done, 1)

            pe.wait_ge(z_stored, FH * B + 4)
            for j in range(PAIRS):
                if j == 1:
                    pe.wait_ge(c2_ready, 1)
                project(j, j % 2)
                if j == 0:
                    pe.wait_ge(c2_row, 1)
                    for u in range(T):
                        last = pe.matmul(bank[7][:, u:u + 1], c_row[0:2, u * P:(u + 1) * P], ones_c[0:2, 0:1],
                                         start=True, stop=True)
                    last.then_inc(c2_mm, 1)
                if 2 <= j < 6:
                    pe.wait_ge(P2_ready, T)
                    u, half = (j - 2) // 2, j % 2
                    last = power(bank[u], u, (2 * half, 2 * half + 1), P2_hi, P2_lo)
                    if half:
                        last.then_inc(P3_mm, 1)
            power(bank[2], 2, range(T), P2_hi, P2_lo).then_inc(P3_mm, 1)

            def y_nodes(c, s):
                pe.wait_ge(y_ready, c + 1)
                pe.wait_ge(r_ready, c + 1)
                for t in range(T):
                    last = pe.transpose(bank[0][:, t * P:(t + 1) * P], y_T[:, s % 2, t * P:(t + 1) * P], ident[:])
                last.then_inc(y_tr, 1)

            def powers_of_x(c, s):
                pe.wait_ge(x1_ready, c + 1)
                pe.wait_ge(U_split, c * 3 + 1)
                for t in range(T):
                    last = pe.transpose(bank[1][:, t * P:(t + 1) * P], X[:, s % 4, t * D:(t + 1) * D], ident[:])
                last.then_inc(U_done, 1)
                pe.wait_ge(x1_split, c + 1)
                for j, (m_hi, m_lo) in enumerate(((PT_hi, PT_lo), (P2_hi, P2_lo))):
                    pe.wait_ge(U_split, c * 3 + (j + 2))
                    for t in range(T):
                        k = slice(t * D, (t + 1) * D)
                        last = split_mm(bank[2 + j], x1_hi[:, s % 2, k], x1_lo[:, s % 2, k], m_hi[:, t],
                                        m_lo[:, t], t == 0, t == T - 1)
                    last.then_inc(U_done, 1)

            def stage_u(c, s, nxt=True):
                if nxt:
                    y_nodes(c + 1, s + 1)
                powers_of_x(c, s)

            def stage_z(c, s):
                pe.wait_ge(U_split, c * 3 + 6)
                for t in range(T):
                    pe.wait_ge(Z_stored, c * T + (t + 1))
                    k = slice(t * P, (t + 1) * P)
                    for j in range(3):
                        last = split_mm(bank[4 + t % 2][:, 0:3 * D], UT_hi[:, s % 2, j, k], UT_lo[:, s % 2, j, k],
                                        G_hi[:, j].rearrange("p a d -> p (a d)"),
                                        G_lo[:, j].rearrange("p a d -> p (a d)"), j == 0, j == 2)
                    last.then_inc(Z_done, 1)

            def times_p3(hi, lo, t, part_ready, need, done):
                for u in range(T):
                    pe.wait_ge(part_ready, need(u))
                    k = slice(t * P, (t + 1) * P)
                    last = split_mm(bank[6 + t % 2], P3_hi[:, u, k], P3_lo[:, u, k], hi(u), lo(u), u == 0, u == T - 1)
                last.then_inc(done, 1)

            def stage_v(g):
                for t in range(T):
                    if t >= 2:
                        pe.wait_ge(V_sum, g * T + (t - 1))
                    else:
                        pe.wait_ge(q_ready, g * T + 1)
                    times_p3(lambda u: Z2_hi[:, u].rearrange("p s d -> p (s d)"),
                             lambda u: Z2_lo[:, u].rearrange("p s d -> p (s d)"), t, Z2_split,
                             lambda u: g * GB + GB, V_done)

            def stage_f(g):
                for t in range(T):
                    if t >= 2:
                        pe.wait_ge(q_ready, g * T + t)
                    else:
                        pe.wait_ge(V_sum, g * T + (t + 3))
                    times_p3(lambda u: V_hi[:, u], lambda u: V_lo[:, u], t, V_split, lambda u: g * T + (u + 1), F_done)

            pe.wait_ge(bn2_ready, 1)
            pe.wait_ge(P3_ready, 2)
            y_nodes(0, 0)
            power(bank[3], 3, range(T), P2_hi, P2_lo).then_inc(P3_mm, 1)
            pe.wait_ge(P3_ready, T)
            pe.wait_ge(G_ready, 1)
            stage_u(0, 0)
            stage_u(1, 1)
            pe.wait_ge(ZB_ready, 1)
            with pe.Fori(0, NG - 1) as g:
                for s in range(GB):
                    stage_z(g * GB + s, s)
                    stage_u(g * GB + (s + 2), s + 2)
                stage_v(g)
                stage_f(g)
            g = NG - 1
            for s in range(GB):
                stage_z(g * GB + s, s)
                if s < 2:
                    stage_u(g * GB + s + 2, s + 2, nxt=s < 1)
            stage_v(g)
            stage_f(g)


_ORDER = ["x", "adj", "L0_gnn_W1", "L0_gnn_b1", "L0_gnn_g1", "L0_gnn_be1", "L0_gnn_W2", "L0_gnn_b2", "L0_gnn_g2",
          "L0_gnn_be2", "L1_gnn_alpha_train", "L1_gnn_w", "L1_gnn_d", "L1_gnn_fc_in_w", "L1_gnn_fc_in_b"]


def kernel(**inputs):
    import numpy as _np
    import concourse.bacc as _bacc
    from concourse import mybir as _mybir
    from concourse.bass_utils import run_bass_kernel_spmd as _run

    nc = _bacc.Bacc("TRN2", target_bir_lowering=False, num_devices=1)
    arrays, args = {}, []
    for name in _ORDER:
        a = _np.ascontiguousarray(inputs[name])
        arrays[f"in_{name}"] = a
        args.append(nc.dram_tensor(f"in_{name}", a.shape, _mybir.dt.from_np(a.dtype), kind="ExternalInput").ap())
    o = nc.dram_tensor("out_0", inputs["x"].shape, F32, kind="ExternalOutput").ap()
    gnn_kernel(nc, *args, o)
    r = _run(nc, [arrays], core_ids=[0])
    return r.results[0]["out_0"]
```

```python
from contextlib import ExitStack
from math import comb

import concourse.bass as bass
from concourse import mybir

F32 = mybir.dt.float32
F32R = mybir.dt.float32r
ALU = mybir.AluOpType
ACT = mybir.ActivationFunctionType
AX = mybir.AxisListType


P = 128
EPS = 1e-5
STEPS = 8
DT = 1.0 / STEPS


def gnn_kernel(nc, x, adj, W1, b1, g1, be1, W2, b2, g2, be2, alpha, w, d, fin_w, fin_b, out):
    B, N, D = x.shape
    H = W1.shape[0]
    T = N // P
    FH = H // P
    GB = 4
    NG = B // GB
    assert D == P and T == 4 and FH == 2 and B % GB == 0 and N == 512

    x_v = x.rearrange("b (p t) d -> b p (t d)", t=T)
    out_v = out.rearrange("b (p t) d -> p b t d", t=T)
    adj_v = adj.rearrange("(p t) m -> p t m", t=T)

    with ExitStack() as ctx:
        base = nc.sbuf_base
        base += -base % 64

        def at(name, kb, shape, dt=F32):
            return nc.alloc_sbuf_tensor_at(name, shape, dt, offset=base + int(kb * 1024))

        zT = at("zT", 0, [P, FH, B, N])
        oT = zT[:, 0]
        A2 = at("A2", 0, [P, T, T, P])
        raw_w1 = at("raw_w1", 60, [P, FH, D])
        raw_w2 = at("raw_w2", 61, [P, H])
        raw_w = at("raw_w", 62, [P, D])
        diag_t = at("diag_t", 56, [P, T, P])
        A_sum = at("A_sum", 54, [P, N])
        junk = at("junk", 44, [P, T, N])
        UT_hi = at("UT_hi", 32, [P, 2, 3, N], F32R)
        UT_lo = at("UT_lo", 44, [P, 2, 3, N], F32R)
        x1_hi = at("x1_hi", 56, [P, 2, N], F32R)
        x1_lo = at("x1_lo", 60, [P, 2, N], F32R)
        PT_hi = at("PT_hi", 64, [P, T, N], F32R)
        PT_lo = at("PT_lo", 72, [P, T, N], F32R)
        P2_hi = at("P2_hi", 80, [P, T, N], F32R)
        P2_lo = at("P2_lo", 88, [P, T, N], F32R)
        Ah_hi = at("Ah_hi", 96, [P, T, N], F32R)
        Ah_lo = at("Ah_lo", 104, [P, T, N], F32R)
        P3_hi = at("P3_hi", 96, [P, T, N], F32R)
        P3_lo = at("P3_lo", 104, [P, T, N], F32R)
        Pn_hi = at("Pn_hi", 112, [P, T, T, P], F32R)
        Pn_lo = at("Pn_lo", 120, [P, T, T, P], F32R)
        Z2_hi = at("Z2_hi", 112, [P, T, GB, D], F32R)
        Z2_lo = at("Z2_lo", 120, [P, T, GB, D], F32R)
        X_hi = at("X_hi", 128, [P, 2, N], F32R)
        X_lo = at("X_lo", 132, [P, 2, N], F32R)
        ag_hi = at("ag_hi", 136, [P, 2, N], F32R)
        ag_lo = at("ag_lo", 140, [P, 2, N], F32R)
        A_n = at("A_n", 144, [P, T, N])
        h_hi = at("h_hi", 128, [P, 2, FH, 2, N], F32R)
        h_lo = at("h_lo", 144, [P, 2, FH, 2, N], F32R)
        V_hi = at("V_hi", 128, [P, T, GB * D], F32R)
        V_lo = at("V_lo", 136, [P, T, GB * D], F32R)
        Z01 = at("Z01", 144, [P, T, GB, 2, D])
        Pn_32 = at("Pn_32", 152, [P, T, T, P])
        X = at("X", 160, [P, 4, N])
        Rp = at("Rp", 168, [P, STEPS + 1, D])
        g_row = at("g_row", 172.5, [P, 3, 3 * D])
        G_32 = at("G_32", 177, [P, 3, 3, D])
        V_32 = at("V_32", 168, [P, 2, GB * D])
        y_out = at("y_out", 172, [P, T, GB, D])
        G_hi = at("G_hi", 181.5, [P, 3, 3, D], F32R)
        G_lo = at("G_lo", 186, [P, 3, 3, D], F32R)
        ZB = at("ZB", 190.5, [P, T, 3 * D])
        W1_hi = at("W1_hi", 196.5, [P, H], F32R)
        W1_lo = at("W1_lo", 197.5, [P, H], F32R)
        W2_hi = at("W2_hi", 198.5, [P, FH, D], F32R)
        W2_lo = at("W2_lo", 199.5, [P, FH, D], F32R)
        y_T = at("y_T", 196.5, [P, 2, N])
        ident = at("ident", 200.5, [P, P])
        raw_f = at("raw_f", 201, [P, D])
        vec = at("vec", 201.5, [P, P])
        wT = at("wT", 202, [P, D])
        wTd = at("wTd", 202.5, [P, D])
        c_row = at("c_row", 201, [P, N])
        Z2 = at("Z2", 201, [P, T, D])
        b_bc = at("b_bc", 203, [P, P])
        g_tmp = at("g_tmp", 203.5, [P, D])
        vecT = at("vecT", 204, [P, 16])
        st1 = at("st1", 204.25, [P, FH, B, 6])
        st2 = at("st2", 205, [P, B, 6])
        ones_c = at("ones_c", 205.5, [P, 2])
        small = at("small", 205.625, [P, 64])
        st_x = at("st_x", 206, [P, T, 6])
        st_y = at("st_y", 206.25, [P, GB, 6])
        c_hl = at("c_hl", 206.5, [P, T, 2], F32R)
        small2 = at("small2", 206.625, [P, 32])
        small3 = at("small3", 206.75, [P, 64])
        assert base + 207 * 1024 <= nc.sbuf_usable_end

        B1, G1, BE1, B2, G2, BE2, DV, FB = 0, 2, 4, 6, 7, 8, 9, 10
        col = lambda k, n=T: small[:, k:k + n]
        rs, cs, dg, deg, sd, dinv, al, c_n, c_d, al_in = (col(4 * i) for i in range(10))
        mv1, v1e, rstd1, s1, t1 = col(40, 4), col(44, 2), col(46, 2), col(48, 2), col(50, 2)
        mv2, v2e, rstd2, s2, t2 = col(52, 2), col(54, 1), col(55, 1), col(56, 1), col(57, 1)
        c1, d_cl, eps_t = col(58, 4), col(62, 1), col(63, 1)
        mvx, sdx, rsx, nmx = small2[:, 0:8], small2[:, 8:12], small2[:, 12:16], small2[:, 16:20]
        c2, ms, sq_warm = small2[:, 20:24], small2[:, 24:28], small2[:, 28:29]
        mvy, sdy, rsy, nmy = ([small3[:, 20 * i + a:20 * i + z] for i in range(2)]
                              for a, z in ((0, 8), (8, 12), (12, 16), (16, 20)))

        wide = [ctx.enter_context(nc.psum_tensor(f"banks{2 * i}", [P, 2, 512], F32)) for i in range(4)]
        bank = [wide[i // 2][:, i % 2] for i in range(8)]

        def sem(name):
            return ctx.enter_context(nc.semaphore(name))

        vec_in, w_in, w12_in, f_in, alpha_in = (sem(n) for n in (
            "vec_in", "w_in", "w12_in", "f_in", "alpha_in"))
        adj_in = [sem(f"adj_in{t}") for t in range(T)]
        x_in = [sem(f"x_in{i}") for i in range(4)]
        out_sent = [sem(f"out_sent{t}") for t in range(T)]
        id_zero, id_ready, consts_ready = sem("id_zero"), sem("id_ready"), sem("consts_ready")
        vec_tr, w_tr, w12_tr, vec_ready, wT_ready, W_hi_ready, W_ready = (sem(n) for n in (
            "vec_tr", "w_tr", "w12_tr", "vec_ready", "wT_ready", "W_hi_ready", "W_ready"))
        A_sum_ready, cs_done, rs_ready, deg_link, deg_ready, sd_ready, dinv_ready = (sem(n) for n in (
            "A_sum_ready", "cs_done", "rs_ready", "deg_link", "deg_ready", "sd_ready", "dinv_ready"))
        diag_ready = sem("diag_ready")
        A2_even, A2_odd, A2_ready, Ah_tr, Ah_hi_ready, Ah_ready = (sem(n) for n in (
            "A2_even", "A2_odd", "A2_ready", "Ah_tr", "Ah_hi_ready", "Ah_ready"))
        al_ready, cn_ready, pool_link, Pn_ready = sem("al_ready"), sem("cn_ready"), sem("pool_link"), sem("Pn_ready")
        Pn_32_ready, Pn_hi_ready, G_sum_ready = sem("Pn_32_ready"), sem("Pn_hi_ready"), sem("G_sum_ready")
        R_mm, R_ready = sem("R_mm"), sem("R_ready")
        X_hi_ready, X_split, agg_done, ag_hi_ready, agg_split = (sem(n) for n in (
            "X_hi_ready", "X_split", "agg_done", "ag_hi_ready", "agg_split"))
        z_done, z_stored, bn_link, bn_sq, bn_sd = (sem(n) for n in ("z_done", "z_stored", "bn_link", "bn_sq", "bn_sd"))
        bn1_ready, bn2_ready = sem("bn1_ready"), sem("bn2_ready")
        h_ready, h_hi_ready, h_hi_act, h_split, o_done, o_stored = (sem(n) for n in (
            "h_ready", "h_hi_ready", "h_hi_act", "h_split", "o_done", "o_stored"))
        PT_tr, PT_hi_ready, PT_ready = sem("PT_tr"), sem("PT_hi_ready"), sem("PT_ready")
        P2_mm, P2_hi_ready, P2_ready = sem("P2_mm"), sem("P2_hi_ready"), sem("P2_ready")
        P3_mm, P3_hi_ready, P3_ready = sem("P3_mm"), sem("P3_hi_ready"), sem("P3_ready")
        F_mm, F_evac = sem("F_mm"), sem("F_evac")
        G_hi_ready, G_ready = sem("G_hi_ready"), sem("G_ready")
        c_link, c2_mm, c2_row, c2_ready = sem("c_link"), sem("c2_mm"), sem("c2_row"), sem("c2_ready")
        ZB_ready = sem("ZB_ready")
        y_ready, y_tr, r_ready, xs_link, x_mom, x_sd, x_rstd, x_norm = (sem(n) for n in (
            "y_ready", "y_tr", "r_ready", "xs_link", "x_mom", "x_sd", "x_rstd", "x_norm"))
        x1_ready, x1_hi_ready, x1_split = sem("x1_ready"), sem("x1_hi_ready"), sem("x1_split")
        x1_first, x1_hi_first, x1_lo_first = sem("x1_first"), sem("x1_hi_first"), sem("x1_lo_first")
        U_done, U_hi_ready, U_split = sem("U_done"), sem("U_hi_ready"), sem("U_split")
        Z_done, Z_stored, Z2_hi_ready, Z2_split = sem("Z_done"), sem("Z_stored"), sem("Z2_hi_ready"), sem("Z2_split")
        V_done, V_sum, V_hi_ready, V_split = sem("V_done"), sem("V_sum"), sem("V_hi_ready"), sem("V_split")
        last_ready = sem("last_ready")
        F_done, q_ready, ys_link, y_mom, y_sd, y_rstd, y_norm, out_ready = (sem(n) for n in (
            "F_done", "q_ready", "ys_link", "y_mom", "y_sd", "y_rstd", "y_norm", "out_ready"))

        block = ctx.enter_context(nc.Block())

        HEAD = 4
        PAIRS = B // 2
        EXTRA = {(0, "a"): ("R", 2), (0, "h"): ("R", 3), (1, "a"): ("R", 5), (1, "h"): ("F", 0), (2, "a"): ("F", 1),
                 (2, "h"): ("F", 2), (3, "a"): ("F", 3), (3, "h"): ("F", 4), (4, "h"): ("F", 5)}
        U_bank = lambda j, late=True: bank[(0 if late else 7, 2, 3)[j]]
        Z_bank = lambda t: bank[(4, 5, 1, 3)[t]]
        P3_bank = lambda u: bank[(0, 2, 3, 6)[u]]
        PT_bank = lambda u: bank[7 - u % 2]
        extra_bank = lambda key: bank[6 + list(EXTRA).index(key) % 2]

        @block.sync
        def _(sp):
            for t in (0, 2):
                sp.dma_start(A_n[:, t], adj_v[:, t]).then_inc(adj_in[t], 16)
            for s in range(2):
                sp.dma_start(X[:, s], x_v[s]).then_inc(x_in[s], 16)
            sp.dma_start(raw_w[:], w).then_inc(w_in, 16)
            sp.dma_start(raw_w1[:], W1.rearrange("(f p) d -> p f d", p=P)).then_inc(w12_in, 16)
            sp.dma_start(raw_w2[:], W2).then_inc(w12_in, 16)
            sp.wait_ge(id_zero, 2)
            for row, v in ((B1, b1), (G1, g1), (BE1, be1)):
                sp.dma_start(vec[row:row + FH, :], v.rearrange("(f p) -> f p", p=P)).then_inc(vec_in, 16)
            for row, v in ((B2, b2), (G2, g2), (BE2, be2), (DV, d), (FB, fin_b)):
                sp.dma_start(vec[row:row + 1, :], v.rearrange("(a p) -> a p", a=1)).then_inc(vec_in, 16)
            for s in range(2, 4):
                sp.dma_start(X[:, s], x_v[s]).then_inc(x_in[s], 16)
            sp.dma_start(raw_f[:], fin_w).then_inc(f_in, 16)
            with sp.Fori(1, B // 4) as i:
                for s in range(4):
                    sp.wait_ge(X_split, i * 4 + (s - 3))
                    sp.dma_start(X[:, s], x_v[i * 4 + s]).then_inc(x_in[s], 16)
            for s in range(4):
                sp.wait_ge(X_split, B - 3 + s)
                sp.dma_start(X[:, s], x_v[s]).then_inc(x_in[s], 16)

            def send(g, end=False):
                for t in range(T):
                    if end and t == T - 1:
                        for e in range(2):
                            sp.wait_ge(last_ready, e + 1)
                            sp.dma_start(out_v[:, g * GB + 2 * e:g * GB + 2 * e + 2, t, :],
                                         y_out[:, t, 2 * e:2 * e + 2]).then_inc(out_sent[t], 16)
                        return
                    sp.wait_ge(out_ready, g * T + (t + 1))
                    sp.dma_start(out_v[:, bass.ds(g * GB, GB), t, :], y_out[:, t]).then_inc(out_sent[t], 16)

            with sp.Fori(1, NG) as g:
                for s in range(4):
                    sp.wait_ge(U_done, (g * 4 + (s - 3)) * 3)
                    sp.dma_start(X[:, s], x_v[g * 4 + s]).then_inc(x_in[s], 16)
                send(g - 1)
            send(NG - 1, end=True)
            for t in range(T):
                sp.wait_ge(out_sent[t], 16 * (NG + 1 + (t == T - 1)))

        @block.gpsimd
        def _(pool):
            pool.memset(ident[:], 0.0).then_inc(id_zero, 1)
            pool.memset(vec[:], 0.0).then_inc(id_zero, 1)
            pool.wait_ge(id_zero, 2)
            pool.affine_select(out=ident[:], in_=ident[:], compare_op=ALU.not_equal, fill=1.0, base=0,
                               pattern=[[-1, P]], channel_multiplier=1).then_inc(id_ready, 1)
            pool.memset(ones_c[:], 1.0)
            pool.memset(eps_t, EPS).then_inc(consts_ready, 1)
            link = 0
            pool.wait_ge(id_ready, 1)
            for t in range(T):
                pool.wait_ge(adj_in[t], 16)
                last = pool.tensor_tensor(diag_t[:, t], A_n[:, t].rearrange("p (q u) -> p u q", u=T)[:, t], ident[:],
                                          ALU.mult)
            last.then_inc(diag_ready, 1)
            pool.wait_ge(cn_ready, 2)
            for t in range(T):
                last = pool.tensor_scalar(Pn_32[:, t], A_n[:, t].rearrange("p (q u) -> p u q", u=T),
                                          c_n[:, t:t + 1], 1.0, ALU.mult, ALU.mult)
            last.then_inc(pool_link, 1)
            link += 1
            for t in range(T):
                pool.wait_ge(pool_link, link)
                pool.wait_ge(id_ready, 1)
                pool.tensor_scalar(g_tmp[:], ident[:], c_d[:, t:t + 1], 1.0, ALU.mult, ALU.mult).then_inc(pool_link, 1)
                link += 1
                pool.wait_ge(pool_link, link)
                pool.tensor_tensor(Pn_32[:, t, t], Pn_32[:, t, t], g_tmp[:],
                                   ALU.add).then_inc(pool_link if t < T - 1 else Pn_32_ready, 1)
                link += 1
            pool.wait_ge(Pn_32_ready, 1)
            link -= 1
            pool.wait_ge(F_evac, 9)
            for k in range(STEPS):
                for m in range(STEPS - k):
                    coef = DT * comb(m + k, k) + (1.0 if k == 0 and m == 0 else 0.0)
                    src = ident[:] if m == 0 else Rp[:, m]
                    pool.wait_ge(pool_link, link)
                    pool.tensor_scalar(g_tmp[:], src, coef, 1.0, ALU.mult, ALU.mult).then_inc(pool_link, 1)
                    link += 1
                    pool.wait_ge(pool_link, link)
                    dst = G_32[:, k % 3, k // 3]
                    pool.tensor_tensor(dst, dst, g_tmp[:],
                                       ALU.add).then_inc(pool_link if k < STEPS - 1 else G_sum_ready, 1)
                    link += 1

        @block.scalar
        def _(act):
            act.dma_start(al_in, alpha.rearrange("(p t) -> p t", t=T)).then_inc(alpha_in, 16)
            for t in (1, 3):
                act.dma_start(A_n[:, t], adj_v[:, t]).then_inc(adj_in[t], 16)
            act.wait_ge(alpha_in, 16)
            act.activation(al, al_in, ACT.Sigmoid).then_inc(al_ready, 1)
            act.wait_ge(consts_ready, 1)
            act.activation(sq_warm, eps_t, ACT.Sqrt)
            for t in range(T):
                act.wait_ge(adj_in[t], 16)
                last = act.activation(junk[:, t], A_n[:, t], ACT.Copy, accum_out=rs[:, t:t + 1])
            last.then_inc(rs_ready, 1)
            for b in range(2):
                act.wait_ge(x_in[b], 16)
                act.activation(X_hi[:, b], X[:, b], ACT.Copy).then_inc(X_hi_ready, 1)
            act.wait_ge(deg_ready, 1)
            act.activation(sd, deg, ACT.Sqrt).then_inc(sd_ready, 1)
            act.wait_ge(dinv_ready, 1)
            for t in (1, 3):
                act.activation(A2[:, t], A_n[:, t].rearrange("p (q u) -> p u q", u=T), ACT.Copy,
                               scale=dinv[:, t:t + 1]).then_inc(A2_odd, 1)
            for t in range(T):
                act.wait_ge(Ah_tr, t + 1)
                act.activation(Ah_hi[:, t], bank[t], ACT.Copy, scale=dinv[:, t:t + 1]).then_inc(Ah_hi_ready, 1)
            act.wait_ge(w12_tr, 1)
            act.activation(W1_hi[:], bank[5][:, 0:H], ACT.Copy)
            act.activation(W2_hi[:].rearrange("p f d -> p (f d)"), bank[5][:, H:2 * H],
                           ACT.Copy).then_inc(W_hi_ready, 1)
            act.sem_inc(z_stored, 4)
            act.wait_ge(vec_ready, 1)

            def extra(key):
                kind, j = EXTRA.get(key, ("", 0))
                if kind != "F":
                    return
                act.wait_ge(F_mm, j + 1)
                for m in range(3 * (j % 3), 3 * (j % 3) + 3):
                    k = STEPS - m
                    dst = G_32[:, k % 3, k // 3] if j < 3 else g_row[:, k % 3, (k // 3) * D:(k // 3 + 1) * D]
                    act.activation(dst, extra_bank(key)[:, (m % 3) * D:(m % 3 + 1) * D], ACT.Copy,
                                   scale=float(comb(STEPS, k))).then_inc(F_evac, 1)

            def agg_high(b, s):
                act.wait_ge(agg_done, b + 1)
                act.activation(ag_hi[:, s % 2], bank[s % 2], ACT.Copy).then_inc(ag_hi_ready, 1)

            def layer1(b, s, x_wait, more=True, head=False, beside=None):
                if s != 3 or more:
                    agg_high(b, s)
                if more:
                    act.wait_ge(x_in[(s + 2) % 4], x_wait)
                    act.activation(X_hi[:, s % 2], X[:, (s + 2) % 4], ACT.Copy).then_inc(X_hi_ready, 1)
                if head:
                    extra((b, "a"))
                if beside:
                    beside()
                if s == 2 and not more:
                    agg_high(B - 1, 3)
                for f in range(FH):
                    act.wait_ge(z_done, b * FH + (f + 1))
                    act.activation(zT[:, f, b, :], bank[2 + FH * (s % 2) + f], ACT.Identity,
                                   bias=vecT[:, B1 + f:B1 + f + 1]).then_inc(z_stored, 1)
                if head:
                    extra((b, "h"))

            def p_high(t):
                act.wait_ge(Pn_32_ready, 1)
                act.activation(Pn_hi[:, t], Pn_32[:, t], ACT.Copy).then_inc(Pn_hi_ready, 1)

            def g_high():
                act.wait_ge(G_sum_ready, 1)
                act.activation(G_hi[:], G_32[:], ACT.Copy).then_inc(G_hi_ready, 1)

            for s in range(HEAD):
                layer1(s, s, (1 + (s + 2) // 4) * 16, head=True)
            with act.Fori(1, B // 4 - 1) as i:
                for s in range(4):
                    layer1(i * 4 + s, s, (i + 1 + (s + 2) // 4) * 16,
                           beside=(lambda: p_high(i * 2 + (s // 2 - 2))) if s % 2 else None)
            for s in range(4):
                layer1(B - 4 + s, s, B // 4 * 16, more=s < 2, beside=g_high if s == 1 else None)
                if s == 0:
                    extra((HEAD, "h"))
                act.wait_ge(PT_tr, s + 1)
                act.activation(PT_hi[:, s], PT_bank(s), ACT.Copy).then_inc(PT_hi_ready, 1)
            act.wait_ge(bn_sq, 1)
            act.activation(v1e, mv1.rearrange("p (f two) -> p f two", two=2)[:, :, 1], ACT.Sqrt,
                           bias=eps_t).then_inc(bn_sd, 1)

            def relu(j, s):
                for f in (1, 0):
                    z = zT[:, f, bass.ds(j * 2, 2), :]
                    act.activation(z, z, ACT.Relu, bias=t1[:, f:f + 1], scale=s1[:, f:f + 1]).then_inc(h_ready, 1)

            def h_high(j, s):
                act.wait_ge(h_ready, j * 2 + 1)
                act.nop(nofuse=True)
                act.activation(h_hi[:, s, 1], zT[:, 1, bass.ds(j * 2, 2), :], ACT.Copy).then_inc(h_hi_act, 1)

            def store_o(j, s):
                act.wait_ge(o_done, j + 1)
                act.activation(oT[:, bass.ds(j * 2, 2), :], wide[2 + s][:], ACT.Identity,
                               bias=vecT[:, B2:B2 + 1]).then_inc(o_stored, 1)

            act.wait_ge(bn1_ready, 1)
            act.sem_inc(o_stored, 2)

            def p2_high(t):
                act.wait_ge(P2_mm, t + 1)
                act.activation(P2_hi[:, t], bank[t], ACT.Copy).then_inc(P2_hi_ready, 1)

            for s in range(2):
                relu(s, s)
                h_high(s, s)
                p2_high(s)

            def p3_high(t):
                act.wait_ge(P3_mm, t + 1)
                act.activation(P3_hi[:, t], P3_bank(t), ACT.Copy).then_inc(P3_hi_ready, 1)

            def pairs(i, s):
                relu(i * 2 + (s + 2), s)
                store_o(i * 2 + s, s)
                h_high(i * 2 + (s + 2), s)

            for s in range(2):
                pairs(0, s)
                p2_high(s + 2)
            with act.Fori(1, PAIRS // 2 - 1) as i:
                for s in range(2):
                    pairs(i, s)
            store_o(PAIRS - 2, 0)
            p3_high(0)
            for e in range(2):
                act.wait_ge(o_done, PAIRS + e)
                act.activation(oT[:, B - 2 + e, :], wide[3][:, e], ACT.Identity,
                               bias=vecT[:, B2:B2 + 1]).then_inc(o_stored, 1)
            act.wait_ge(bn_sq, 2)
            act.activation(v2e, mv2[:, 1:2], ACT.Sqrt, bias=eps_t).then_inc(bn_sd, 1)
            p3_high(1)
            act.wait_ge(bn2_ready, 1)

            def affine(c, s):
                act.activation(y_T[:, s % 2], oT[:, c, :], ACT.Identity, bias=t2, scale=s2).then_inc(y_ready, 1)

            def root(c):
                act.wait_ge(x_mom, c + 1)
                act.activation(sdx, mvx.rearrange("p (t two) -> p t two", two=2)[:, :, 1], ACT.Sqrt,
                               bias=eps_t).then_inc(x_sd, 1)

            def normalize(c, s):
                act.wait_ge(x_norm, c + 1)
                for t in range(T):
                    part = X[:, s % 4, t * D:(t + 1) * D]
                    last = act.activation(part, part, ACT.Identity, bias=nmx[:, t:t + 1], scale=rsx[:, t:t + 1])
                last.then_inc(x1_ready, 1)

            def x1_high(c, s):
                act.wait_ge(x1_ready, c + 1)
                act.activation(x1_hi[:, s % 2], X[:, s % 4], ACT.Copy).then_inc(x1_hi_ready, 1)

            def u_high(c, s, j, late=True):
                act.wait_ge(U_done, c * 3 + (j + 2) % 3 + 1)
                act.activation(UT_hi[:, s % 2, j], U_bank(j, late), ACT.Copy).then_inc(U_hi_ready, 1)

            def stage_u(c, s, nxt=True, nxt2=True):
                if nxt2:
                    affine(c + 2, s)
                if nxt:
                    root(c + 1)
                u_high(c, s, 1)
                if nxt:
                    normalize(c + 1, s + 1)
                u_high(c, s, 2)
                u_high(c, s, 0)
                if nxt:
                    x1_high(c + 1, s + 1)

            def stage_z(c, s):
                act.wait_ge(Z_stored, c * T + (T + 4))
                act.activation(Z2_hi[:, :, s % GB, :], Z2[:], ACT.Copy).then_inc(Z2_hi_ready, 1)

            def stage_z_last():
                for t in range(T):
                    act.wait_ge(Z_stored, (B - 1) * T + (t + 5))
                    act.activation(Z2_hi[:, t, GB - 1, :], Z2[:, t], ACT.Copy).then_inc(Z2_hi_ready, 1)

            def stage_v(g):
                for t in range(T):
                    act.wait_ge(V_sum, g * T + (t + 1))
                    act.activation(V_hi[:, t], V_32[:, t % 2], ACT.Copy).then_inc(V_hi_ready, 1)

            def out_root(g, t):
                act.wait_ge(y_mom, g * T + (t + 1))
                act.activation(sdy[t % 2], mvy[t % 2].rearrange("p (t two) -> p t two", two=2)[:, :, 1], ACT.Sqrt,
                               bias=eps_t).then_inc(y_sd, 1)

            def out_normalize(g, t):
                act.wait_ge(y_norm, g * T + (t + 1))
                for s in range(GB):
                    part = y_out[:, t, s]
                    last = act.activation(part, part, ACT.Identity, bias=nmy[t % 2][:, s:s + 1],
                                          scale=rsy[t % 2][:, s:s + 1])
                last.then_inc(out_ready, 1)

            def stage_f(g, end=False):
                for t in range(T):
                    out_root(g, t)
                    if t:
                        out_normalize(g, t - 1)
                if not end:
                    out_normalize(g, T - 1)

            affine(0, 0)
            affine(1, 1)
            p3_high(2)
            root(0)

            def first_x1_high(c):
                for t in range(T):
                    k = slice(t * D, (t + 1) * D)
                    act.wait_ge(x1_first, c * T + t + 1)
                    act.activation(x1_hi[:, c, k], X[:, c, k], ACT.Copy).then_inc(x1_hi_first, 1)

            first_x1_high(0)
            act.sem_inc(x1_ready, 2)
            act.sem_inc(x1_hi_ready, 2)
            p3_high(3)
            affine(2, 2)
            root(1)
            u_high(0, 0, 1)
            first_x1_high(1)
            u_high(0, 0, 2)
            u_high(0, 0, 0, late=False)
            affine(3, 3)
            root(2)
            u_high(1, 1, 1)
            normalize(2, 2)
            x1_high(2, 2)
            u_high(1, 1, 2)
            u_high(1, 1, 0, late=False)
            with act.Fori(0, NG - 1) as g:
                for s in range(GB):
                    stage_z(g * GB + s, s)
                    stage_u(g * GB + (s + 2), s + 2)
                stage_v(g)
                stage_f(g)
            g = NG - 1
            for s in range(GB - 1):
                stage_z(g * GB + s, s)
                if s < 2:
                    stage_u(g * GB + s + 2, s + 2, nxt=s < 1, nxt2=False)
            stage_z_last()
            stage_v(g)
            stage_f(g, end=True)

        @block.vector
        def _(dve):
            dve.wait_ge(adj_in[0], 16)
            for t in range(1, T):
                dve.wait_ge(adj_in[t], 16)
                if t > 1:
                    dve.wait_ge(A_sum_ready, t - 1)
                dve.tensor_tensor(A_sum[:], A_n[:, 0] if t == 1 else A_sum[:], A_n[:, t],
                                  ALU.add).then_inc(A_sum_ready, 1)
            dve.wait_ge(diag_ready, 1)
            dve.reduce_sum(dg, diag_t[:], AX.X).then_inc(deg_link, 1)
            dve.wait_ge(rs_ready, 1)
            dve.wait_ge(deg_link, 1)
            dve.tensor_tensor(cs, rs, dg, ALU.subtract).then_inc(deg_link, 1)
            dve.wait_ge(al_ready, 1)
            dve.tensor_scalar(c_n, al, DT * 0.5, None, ALU.mult).then_inc(cn_ready, 1)
            dve.tensor_scalar(c_d, al, -DT * 0.5, 1.0 - DT, ALU.mult, ALU.add).then_inc(cn_ready, 1)
            dve.wait_ge(cs_done, 1)
            dve.wait_ge(deg_link, 2)
            dve.scalar_tensor_tensor(out=deg, in0=bank[4][:, 0:T], scalar=1.0, in1=cs, op0=ALU.add,
                                     op1=ALU.add).then_inc(deg_ready, 1)
            dve.wait_ge(sd_ready, 1)
            dve.reciprocal(dinv, sd).then_inc(dinv_ready, 1)
            dve.wait_ge(dinv_ready, 1)
            for t in range(T):
                if t % 2 == 0:
                    dve.tensor_scalar(A2[:, t], A_n[:, t].rearrange("p (q u) -> p u q", u=T), dinv[:, t:t + 1],
                                      None, ALU.mult).then_inc(A2_even, 1)
                dve.wait_ge(A2_odd if t % 2 else A2_even, t // 2 + 1)
                dve.scalar_tensor_tensor(out=A2[:, t, t], in0=ident[:], scalar=dinv[:, t:t + 1],
                                         in1=A2[:, t, t], op0=ALU.mult, op1=ALU.add).then_inc(A2_ready, 1)
            for b in range(2):
                dve.wait_ge(X_hi_ready, b + 1)
                dve.tensor_tensor(X_lo[:, b], X[:, b], X_hi[:, b].bitcast(F32), ALU.subtract).then_inc(X_split, 1)
            dve.sem_inc(agg_split, 2)
            dve.wait_ge(cn_ready, 2)
            for t in range(T):
                last = dve.scalar_tensor_tensor(out=c1[:, t:t + 1], in0=rs[:, t:t + 1], scalar=c_n[:, t:t + 1],
                                                in1=c_d[:, t:t + 1], op0=ALU.mult, op1=ALU.add)
            last.then_inc(c_link, 1)
            dve.wait_ge(c_link, 1)
            dve.tensor_copy(c_hl[:, :, 0], c1).then_inc(c_link, 1)
            dve.wait_ge(c_link, 2)
            dve.tensor_tensor(c_hl[:, :, 1], c1, c_hl[:, :, 0].bitcast(F32), ALU.subtract).then_inc(c_link, 1)
            for t in range(T):
                dve.wait_ge(Ah_hi_ready, t + 1)
                dve.scalar_tensor_tensor(out=Ah_lo[:, t], in0=bank[t], scalar=dinv[:, t:t + 1],
                                         in1=Ah_hi[:, t].bitcast(F32), op0=ALU.mult,
                                         op1=ALU.subtract).then_inc(Ah_ready, 1)
            dve.wait_ge(vec_tr, 1)
            dve.tensor_copy(vecT[:], bank[6][:, 0:16]).then_inc(vec_ready, 1)
            dve.wait_ge(vec_ready, 1)
            dve.tensor_scalar(d_cl, vecT[:, DV:DV + 1], 0.0, 1.0, ALU.max, ALU.min)
            dve.wait_ge(w_tr, 1)
            dve.tensor_copy(wT[:], bank[7][:, 0:D]).then_inc(wT_ready, 1)
            dve.wait_ge(wT_ready, 1)
            dve.tensor_scalar(wTd[:], wT[:], d_cl, None, ALU.mult).then_inc(wT_ready, 1)
            dve.wait_ge(W_hi_ready, 1)
            dve.tensor_tensor(W1_lo[:], bank[5][:, 0:H], W1_hi[:].bitcast(F32), ALU.subtract).then_inc(W_ready, 1)
            dve.tensor_tensor(W2_lo[:].rearrange("p f d -> p (f d)"), bank[5][:, H:2 * H],
                              W2_hi[:].rearrange("p f d -> p (f d)").bitcast(F32), ALU.subtract).then_inc(W_ready, 1)
            dve.wait_ge(R_mm, 1)
            dve.tensor_scalar(Rp[:, 1], bank[7][:, 0:D], DT, None, ALU.mult).then_inc(R_ready, 1)
            dve.tensor_scalar(Rp[:, 0], ident[:], 1.0, None, ALU.mult).then_inc(R_ready, 1)
            dve.tensor_scalar(b_bc[:], ident[:], 0.0, vecT[:, FB:FB + 1], ALU.mult, ALU.add).then_inc(R_ready, 1)

            powers = {2: (2, 3, 2), 3: (3, 5, 3), 5: (5, 9, 4)}

            def extra(key):
                kind, j = EXTRA.get(key, ("", 0))
                if kind == "R":
                    a, z, n = powers[j]
                    dve.wait_ge(R_mm, n)
                    dve.tensor_copy(Rp[:, a:z].rearrange("p m d -> p (m d)"),
                                    extra_bank(key)[:, 0:(z - a) * D]).then_inc(R_ready, 1)

            def pt_low(t):
                dve.wait_ge(PT_hi_ready, t + 1)
                dve.tensor_tensor(PT_lo[:, t], PT_bank(t), PT_hi[:, t].bitcast(F32), ALU.subtract).then_inc(PT_ready, 1)

            def agg_low(b, s):
                dve.wait_ge(ag_hi_ready, b + 1)
                dve.tensor_tensor(ag_lo[:, s % 2], bank[s % 2], ag_hi[:, s % 2].bitcast(F32),
                                  ALU.subtract).then_inc(agg_split, 1)

            def layer1(b, s, more=True, head=False, beside=None):
                if s != 3 or more:
                    agg_low(b, s)
                if more:
                    dve.wait_ge(X_hi_ready, b + 3)
                    dve.tensor_tensor(X_lo[:, s % 2], X[:, (s + 2) % 4], X_hi[:, s % 2].bitcast(F32),
                                      ALU.subtract).then_inc(X_split, 1)
                if head:
                    extra((b, "a"))
                if beside:
                    beside()
                if s == 2 and not more:
                    agg_low(B - 1, 3)
                if not more:
                    pt_low(s - 1)
                for f in range(FH):
                    dve.wait_ge(z_stored, b * FH + (f + 1 + 4))
                    last = dve.bn_stats(st1[:, f, b, :], zT[:, f, b, :])
                if not more:
                    last.then_inc(bn_link, 1)
                if head:
                    extra((b, "h"))

            def p_low(t):
                dve.wait_ge(Pn_hi_ready, t + 1)
                dve.tensor_tensor(Pn_lo[:, t], Pn_32[:, t], Pn_hi[:, t].bitcast(F32),
                                  ALU.subtract).then_inc(Pn_ready, 1)

            def zb_first(tiles):
                dve.wait_ge(F_evac, 18)
                for t in tiles:
                    dve.scalar_tensor_tensor(out=ZB[:, t], in0=g_row[:, 1], scalar=c1[:, t:t + 1],
                                             in1=g_row[:, 0], op0=ALU.mult, op1=ALU.add)

            for s in range(HEAD):
                layer1(s, s, head=True)
            with dve.Fori(1, B // 4 - 1) as i:
                for s in range(4):
                    layer1(i * 4 + s, s, beside=(lambda: p_low(i * 2 + (s // 2 - 2))) if s % 2 else None)
            for s in range(4):
                if s == 1:
                    pt_low(0)
                layer1(B - 4 + s, s, more=s < 2, beside={1: lambda: zb_first((0, 1)),
                                                         2: lambda: zb_first((2, 3))}.get(s))

            dve.wait_ge(bn_link, 2)
            for f in range(FH):
                last = dve.bn_aggr(mv1[:, 2 * f:2 * f + 2], st1[:, f].rearrange("p b k -> p (b k)"))
            last.then_inc(bn_sq, 1)
            pt_low(T - 1)
            dve.wait_ge(bn_sd, 1)
            dve.reciprocal(rstd1, v1e).then_inc(bn_link, 1)
            dve.wait_ge(bn_link, 3)
            dve.tensor_tensor(s1, rstd1, vecT[:, G1:G1 + FH], ALU.mult).then_inc(bn_link, 1)
            dve.wait_ge(bn_link, 4)
            dve.tensor_tensor(ms[:, 0:FH], mv1.rearrange("p (f two) -> p f two", two=2)[:, :, 0], s1,
                              ALU.mult).then_inc(bn_link, 1)
            dve.wait_ge(bn_link, 5)
            dve.tensor_tensor(t1, vecT[:, BE1:BE1 + FH], ms[:, 0:FH], ALU.subtract).then_inc(bn1_ready, 1)
            dve.wait_ge(G_hi_ready, 1)
            dve.tensor_tensor(G_lo[:], G_32[:], G_hi[:].bitcast(F32), ALU.subtract).then_inc(G_ready, 1)

            def split_h(j, s, o_wait=None):
                if o_wait is not None:
                    dve.wait_ge(o_done, o_wait)
                dve.wait_ge(h_ready, j * 2 + 2)
                dve.tensor_copy(h_hi[:, s, 0], zT[:, 0, bass.ds(j * 2, 2), :]).then_inc(h_hi_ready, 1)
                dve.wait_ge(h_hi_ready, j + 1)
                for f in range(FH):
                    if f == 1:
                        dve.wait_ge(h_hi_act, j + 1)
                    last = dve.tensor_tensor(h_lo[:, s, f], zT[:, f, bass.ds(j * 2, 2), :],
                                             h_hi[:, s, f].bitcast(F32), ALU.subtract)
                last.then_inc(h_split, 1)

            def stats_o(j, s):
                dve.wait_ge(o_stored, j + 3)
                for e in range(2):
                    dve.bn_stats(st2[:, j * 2 + e, :], oT[:, j * 2 + e, :])

            def p2_low(t):
                dve.wait_ge(P2_hi_ready, t + 1)
                dve.tensor_tensor(P2_lo[:, t], bank[t], P2_hi[:, t].bitcast(F32), ALU.subtract).then_inc(P2_ready, 1)

            for s in range(2):
                split_h(s, s)
                p2_low(s)

            def p3_low(t):
                dve.wait_ge(P3_hi_ready, t + 1)
                dve.tensor_tensor(P3_lo[:, t], P3_bank(t), P3_hi[:, t].bitcast(F32), ALU.subtract).then_inc(P3_ready, 1)

            for s in range(2):
                split_h(s + 2, s, s + 1)
                stats_o(s, s)
                p2_low(s + 2)
            dve.wait_ge(c2_mm, 1)
            dve.tensor_copy(c_row[0:2], bank[1][0:2]).then_inc(c2_row, 1)
            with dve.Fori(1, PAIRS // 2 - 1) as i:
                for s in range(2):
                    split_h(i * 2 + (s + 2), s, i * 2 + (s + 1))
                    stats_o(i * 2 + s, s)
            dve.wait_ge(c2_mm, 2)
            dve.tensor_copy(c2, bank[3][:, 0:T]).then_inc(c2_ready, 1)
            stats_o(PAIRS - 2, 0)
            p3_low(0)
            for e in range(2):
                dve.wait_ge(o_stored, PAIRS + 2 + e)
                last = dve.bn_stats(st2[:, B - 2 + e, :], oT[:, B - 2 + e, :])
            last.then_inc(bn_link, 1)
            dve.wait_ge(bn_link, 6)
            dve.bn_aggr(mv2, st2[:].rearrange("p b k -> p (b k)")).then_inc(bn_sq, 1)
            dve.wait_ge(bn_sd, 2)
            dve.reciprocal(rstd2, v2e).then_inc(bn_link, 1)
            dve.wait_ge(bn_link, 7)
            dve.tensor_tensor(s2, rstd2, vecT[:, G2:G2 + 1], ALU.mult).then_inc(bn_link, 1)
            dve.wait_ge(bn_link, 8)
            dve.tensor_tensor(ms[:, 2:3], mv2[:, 0:1], s2, ALU.mult).then_inc(bn_link, 1)
            dve.wait_ge(bn_link, 9)
            dve.tensor_tensor(t2, vecT[:, BE2:BE2 + 1], ms[:, 2:3], ALU.subtract).then_inc(bn2_ready, 1)
            dve.sem_inc(r_ready, 1)
            dve.sem_inc(U_split, 3)
            dve.sem_inc(Z_stored, 4)
            dve.sem_inc(q_ready, 1)
            for t in range(T):
                dve.sem_inc(out_sent[t], 16)

            def moments(c, s, x_wait):
                dve.wait_ge(x_in[s % 4], x_wait)
                dve.wait_ge(y_tr, c + 1)
                dve.tensor_tensor(X[:, s % 4], X[:, s % 4], bank[0], ALU.add).then_inc(r_ready, 1)
                dve.wait_ge(r_ready, c + 2)
                for t in range(T):
                    last = dve.bn_stats(st_x[:, t], X[:, s % 4, t * D:(t + 1) * D])
                last.then_inc(xs_link, 1)
                dve.wait_ge(xs_link, c + 1)
                dve.nop(nofuse=True)
                for t in range(T):
                    last = dve.bn_aggr(mvx[:, 2 * t:2 * t + 2], st_x[:, t])
                last.then_inc(x_mom, 1)

            def norm_scale(c):
                dve.wait_ge(x_sd, c + 1)
                dve.reciprocal(rsx, sdx).then_inc(x_rstd, 1)
                dve.wait_ge(x_rstd, c + 1)
                dve.scalar_tensor_tensor(out=nmx, in0=mvx.rearrange("p (t two) -> p t two", two=2)[:, :, 0],
                                         scalar=-1.0, in1=rsx, op0=ALU.mult, op1=ALU.mult).then_inc(x_norm, 1)

            def x1_low(c, s):
                dve.wait_ge(x1_hi_ready, c + 1)
                dve.tensor_tensor(x1_lo[:, s % 2], X[:, s % 4], x1_hi[:, s % 2].bitcast(F32),
                                  ALU.subtract).then_inc(x1_split, 1)

            def u_low(c, s, j, late=True):
                dve.wait_ge(U_hi_ready, c * 3 + (j + 2) % 3 + 1)
                dve.tensor_tensor(UT_lo[:, s % 2, j], U_bank(j, late), UT_hi[:, s % 2, j].bitcast(F32),
                                  ALU.subtract).then_inc(U_split, 1)

            def stage_u(c, s, x_wait=None):
                if x_wait is not None:
                    moments(c + 1, s + 1, x_wait)
                    norm_scale(c + 1)
                u_low(c, s, 1)
                u_low(c, s, 2)

            def z2_low_tile(t):
                dve.wait_ge(Z2_hi_ready, B + t)
                dve.tensor_tensor(Z2_lo[:, t, GB - 1, :], Z2[:, t], Z2_hi[:, t, GB - 1, :].bitcast(F32),
                                  ALU.subtract).then_inc(Z2_split, 1)

            def stage_z(c, s, rest=(False, False), end=False):
                for t in range(T):
                    if t == 1 and rest[0]:
                        u_low(c + 1, s + 1, 0)
                    if t == 2 and rest[1]:
                        x1_low(c + 2, s + 2)
                    dve.wait_ge(Z_done, c * T + (t + 1))
                    dve.tensor_tensor(Z01[:, t, s % GB].rearrange("p a d -> p (a d)"), Z_bank(t)[:, 0:2 * D],
                                      ZB[:, t, 0:2 * D], ALU.add)
                    dve.tensor_tensor(Z2[:, t], Z_bank(t)[:, 2 * D:3 * D], ZB[:, t, 2 * D:3 * D],
                                      ALU.add).then_inc(Z_stored, 1)
                    if end and t:
                        z2_low_tile(t - 1)
                if end:
                    z2_low_tile(T - 1)
                    return
                dve.wait_ge(Z2_hi_ready, c + 1)
                dve.tensor_tensor(Z2_lo[:, :, s % GB, :], Z2[:], Z2_hi[:, :, s % GB, :].bitcast(F32),
                                  ALU.subtract).then_inc(Z2_split, 1)

            def flush(c, s):
                u_low(c + 1, s + 1, 0)
                x1_low(c + 2, s + 2)

            def v_low(g, t):
                dve.wait_ge(V_hi_ready, g * T + (t + 1))
                dve.tensor_tensor(V_lo[:, t], V_32[:, t % 2], V_hi[:, t].bitcast(F32),
                                  ALU.subtract).then_inc(V_split, 1)

            def stage_v(g):
                for t in range(T):
                    if t >= 2:
                        dve.wait_ge(V_split, g * T + (t - 1))
                    dve.wait_ge(V_done, g * T + (t + 1))
                    dve.tensor_tensor(V_32[:, t % 2].rearrange("p (s d) -> p s d", d=D),
                                      bank[6 + t % 2].rearrange("p (s d) -> p s d", d=D), Z01[:, t, :, 1],
                                      ALU.add).then_inc(V_sum, 1)
                    for u in ((), (0, 1), (2,), (3,))[t]:
                        v_low(g, u)

            def out_scale(g, t):
                dve.wait_ge(y_sd, g * T + (t + 1))
                dve.reciprocal(rsy[t % 2], sdy[t % 2]).then_inc(y_rstd, 1)
                dve.wait_ge(y_rstd, g * T + (t + 1))
                mean = mvy[t % 2].rearrange("p (t two) -> p t two", two=2)[:, :, 0]
                dve.scalar_tensor_tensor(out=nmy[t % 2], in0=mean, scalar=-1.0, in1=rsy[t % 2], op0=ALU.mult,
                                         op1=ALU.mult).then_inc(y_norm, 1)

            def stage_f(g, end=False):
                for t in range(T):
                    if t == 2:
                        out_scale(g, 1)
                    dve.wait_ge(F_done, g * T + (t + 1))
                    dve.wait_ge(out_sent[t], (g + 1) * 16)
                    dve.tensor_tensor(y_out[:, t], bank[6 + t % 2].rearrange("p (s d) -> p s d", d=D),
                                      Z01[:, t, :, 0], ALU.add).then_inc(q_ready, 1)
                    dve.wait_ge(q_ready, g * T + (t + 2))
                    for s in range(GB):
                        last = dve.bn_stats(st_y[:, s], y_out[:, t, s])
                    last.then_inc(ys_link, 1)
                    dve.wait_ge(ys_link, g * T + (t + 1))
                    dve.nop(nofuse=True)
                    for s in range(GB):
                        last = dve.bn_aggr(mvy[t % 2][:, 2 * s:2 * s + 2], st_y[:, s])
                    last.then_inc(y_mom, 1)
                    if t in (1, T - 1):
                        out_scale(g, t - 1)
                if not end:
                    out_scale(g, T - 1)
                else:
                    dve.wait_ge(y_sd, NG * T)
                    dve.reciprocal(rsy[1], sdy[1]).then_inc(y_rstd, 1)
                    dve.wait_ge(y_rstd, NG * T)
                    for s in range(GB):
                        part = y_out[:, T - 1, s]
                        last = dve.tensor_scalar(part, part, mvy[1][:, 2 * s:2 * s + 1], rsy[1][:, s:s + 1],
                                                 ALU.subtract, ALU.mult)
                        if s % 2:
                            last.then_inc(last_ready, 1)

            loads_1 = B // 4
            p3_low(1)

            def first_x1(c):
                dve.wait_ge(x_sd, c + 1)
                dve.reciprocal(rsx, sdx).then_inc(x_rstd, 1)
                dve.wait_ge(x_rstd, c + 1)
                for t in range(T):
                    part = X[:, c, t * D:(t + 1) * D]
                    dve.tensor_scalar(part, part, mvx[:, 2 * t:2 * t + 1], rsx[:, t:t + 1], ALU.subtract,
                                      ALU.mult).then_inc(x1_first, 1)
                for t in range(T):
                    k = slice(t * D, (t + 1) * D)
                    dve.wait_ge(x1_hi_first, c * T + t + 1)
                    dve.tensor_tensor(x1_lo[:, c, k], X[:, c, k], x1_hi[:, c, k].bitcast(F32),
                                      ALU.subtract).then_inc(x1_lo_first, 1)

            moments(0, 0, (loads_1 + 1) * 16)
            first_x1(0)
            p3_low(2)
            moments(1, 1, (loads_1 + 1) * 16)
            u_low(0, 0, 1)
            first_x1(1)
            dve.sem_inc(x1_split, 2)
            dve.sem_inc(x_norm, 2)
            u_low(0, 0, 2)
            u_low(0, 0, 0, late=False)
            p3_low(3)
            moments(2, 2, (loads_1 + 1) * 16)
            norm_scale(2)
            u_low(1, 1, 1)
            dve.wait_ge(c2_ready, 1)
            for t in range(T):
                last = dve.scalar_tensor_tensor(out=ZB[:, t], in0=g_row[:, 2], scalar=c2[:, t:t + 1],
                                                in1=ZB[:, t], op0=ALU.mult, op1=ALU.add)
            last.then_inc(ZB_ready, 1)
            x1_low(2, 2)
            u_low(1, 1, 2)
            u_low(1, 1, 0, late=False)
            dve.wait_ge(ZB_ready, 1)
            with dve.Fori(0, NG - 1) as g:
                for s in range(GB):
                    stage_z(g * GB + s, s, (s > 0, s > 0))
                    stage_u(g * GB + (s + 2), s + 2, (g + (loads_1 + 1 + (s + 3) // 4)) * 16)
                flush(g * GB + GB, GB)
                stage_v(g)
                stage_f(g)
            g = NG - 1
            for s in range(GB):
                if s:
                    dve.wait_ge(Z2_split, g * GB + s)
                stage_z(g * GB + s, s, (s in (1, 2), s == 1), end=s == GB - 1)
                if s < 2:
                    stage_u(g * GB + s + 2, s + 2, (loads_1 + NG) * 16 if s < 1 else None)
            stage_v(g)
            stage_f(g, end=True)

        @block.tensor
        def _(pe):
            def split_mm(dst, w_hi, w_lo, m_hi, m_lo, first, last):
                pe.matmul(dst, w_hi, m_hi, start=first, stop=False)
                pe.matmul(dst, w_hi, m_lo, start=False, stop=False)
                return pe.matmul(dst, w_lo, m_hi, start=False, stop=last)

            pe.wait_ge(A_sum_ready, T - 1)
            pe.wait_ge(consts_ready, 1)
            for u in range(T):
                last = pe.matmul(bank[4][:, u:u + 1], A_sum[:].rearrange("p (q u) -> p u q", u=T)[:, u],
                                 ones_c[:, 0:1], start=True, stop=True)
            last.then_inc(cs_done, 1)
            pe.wait_ge(id_ready, 1)
            pe.wait_ge(w_in, 16)
            pe.transpose(bank[7][:, 0:P], raw_w[:], ident[:]).then_inc(w_tr, 1)
            pe.wait_ge(w12_in, 2 * 16)
            for f in range(FH):
                pe.transpose(bank[5][:, f * P:(f + 1) * P], raw_w1[:, f], ident[:])
            for f in range(FH):
                last = pe.transpose(bank[5][:, H + f * P:H + (f + 1) * P], raw_w2[:, f * P:(f + 1) * P], ident[:])
            last.then_inc(w12_tr, 1)
            for t in range(T):
                pe.wait_ge(A2_ready, t + 1)
                for u in range(T):
                    last = pe.transpose(bank[u][:, t * P:(t + 1) * P], A2[:, t, u], ident[:])
                    if t == T - 1:
                        last.then_inc(Ah_tr, 1)
            pe.wait_ge(vec_in, 8 * 16)
            pe.transpose(bank[6][:, 0:P], vec[:], ident[:]).then_inc(vec_tr, 1)

            def aggregate(b, s, first=False):
                pe.wait_ge(X_split, b + 1)
                pe.wait_ge(agg_split, b + 1)
                for t in range(T):
                    if first:
                        pe.wait_ge(Ah_ready, t + 1)
                    k = slice(t * D, (t + 1) * D)
                    last = split_mm(bank[s % 2], X_hi[:, s % 2, k], X_lo[:, s % 2, k], Ah_hi[:, t], Ah_lo[:, t],
                                    t == 0, t == T - 1)
                last.then_inc(agg_done, 1)

            def hidden(b, s):
                pe.wait_ge(agg_split, b + 3)
                for f in range(FH):
                    pe.wait_ge(z_stored, b * FH + (f + 1))
                    k = slice(f * P, (f + 1) * P)
                    split_mm(bank[2 + FH * (s % 2) + f], W1_hi[:, k], W1_lo[:, k], ag_hi[:, s % 2],
                             ag_lo[:, s % 2], True, True).then_inc(z_done, 1)

            def extra(key):
                if key not in EXTRA:
                    return
                kind, j = EXTRA[key]
                dst = extra_bank(key)
                if kind == "R":
                    a, lhs, need = {2: (1, 1, 1), 3: (1, 2, 4), 5: (1, 4, 5)}[j]
                    z = {2: 2, 3: 3, 5: 5}[j]
                    pe.wait_ge(R_ready, need)
                    pe.matmul(dst[:, 0:(z - a) * D], Rp[:, lhs], Rp[:, a:z].rearrange("p m d -> p (m d)"),
                              start=True, stop=True).then_inc(R_mm, 1)
                else:
                    pe.wait_ge(R_ready, 6)
                    pe.wait_ge(f_in, 16)
                    if j >= 2:
                        pe.wait_ge(F_evac, 3 * (j - 1))
                    m = 3 * (j % 3)
                    pe.matmul(dst[:, 0:3 * D], raw_f[:] if j < 3 else b_bc[:],
                              Rp[:, m:m + 3].rearrange("p m d -> p (m d)"), start=True, stop=True).then_inc(F_mm, 1)

            aggregate(0, 0, first=True)
            pe.wait_ge(wT_ready, 2)
            pe.matmul(bank[7][:, 0:D], wTd[:], wT[:], start=True, stop=True).then_inc(R_mm, 1)
            pe.wait_ge(W_ready, 2)
            for s in range(HEAD):
                aggregate(s + 1, s + 1)
                extra((s, "a"))
                hidden(s, s)
                extra((s, "h"))

            def p_transposed(u):
                for t in range(T):
                    last = pe.transpose(PT_bank(u)[:, t * P:(t + 1) * P], Pn_32[:, t, u], ident[:])
                last.then_inc(PT_tr, 1)

            with pe.Fori(HEAD // 2, B // 2 - 2) as i:
                for s in range(2):
                    aggregate(i * 2 + (s + 1), s + 1)
                    hidden(i * 2 + s, s)
            pe.wait_ge(Pn_32_ready, 1)
            for s in range(4):
                if s < 3:
                    aggregate(B - 3 + s, s + 1)
                else:
                    pe.wait_ge(PT_ready, 2)
                    p_transposed(3)
                hidden(B - 4 + s, s)
                if s == 0:
                    extra((HEAD, "h"))
                    pe.wait_ge(F_evac, 15)
                    p_transposed(0)
                elif s == 1:
                    pe.wait_ge(F_evac, 18)
                    p_transposed(1)
                elif s == 2:
                    pe.wait_ge(PT_ready, 1)
                    p_transposed(2)

            def power(dst, u, parts, src_hi, src_lo):
                for t in parts:
                    last = split_mm(dst, Pn_hi[:, t, u], Pn_lo[:, t, u], src_hi[:, t], src_lo[:, t],
                                    t == 0, t == T - 1)
                return last

            def project(j, s):
                pe.wait_ge(h_split, j + 1)
                pe.wait_ge(o_stored, j + 1)
                for e in range(2):
                    for f in range(FH):
                        last = split_mm(wide[2 + s][:, e], W2_hi[:, f], W2_lo[:, f], h_hi[:, s, f, e],
                                        h_lo[:, s, f, e], f == 0, f == FH - 1)
                    if j == PAIRS - 1 and e == 0:
                        last.then_inc(o_done, 1)
                last.then_inc(o_done, 1)

            def p_square(u):
                for t in range(T):
                    if u == 0:
                        pe.wait_ge(PT_ready, t + 1)
                    last = power(bank[u], u, (t,), PT_hi, PT_lo)
                last.then_inc(P2_mm, 1)

            pe.wait_ge(Pn_ready, T)
            pe.wait_ge(agg_split, B + 2)
            p_square(0)
            p_square(1)
            pe.wait_ge(z_stored, FH * (B - 1) + 4)
            p_square(2)
            pe.wait_ge(z_stored, FH * B + 4)
            for j in range(PAIRS):
                project(j, j % 2)
                if j == 0:
                    p_square(3)
                elif j == 1:
                    pe.wait_ge(P2_ready, 2)
                    pe.wait_ge(c_link, 3)
                    for t in range(T):
                        pe.matmul(bank[1][0:2], c_hl[:, t], PT_hi[:, t], start=t == 0, stop=False)
                        last = pe.matmul(bank[1][0:2], c_hl[:, t], PT_lo[:, t], start=False, stop=t == T - 1)
                    last.then_inc(c2_mm, 1)
                elif j == 4:
                    pe.wait_ge(c2_row, 1)
                    for u in range(T):
                        last = pe.matmul(bank[3][:, u:u + 1], c_row[0:2, u * P:(u + 1) * P], ones_c[0:2, 0:1],
                                         start=True, stop=True)
                    last.then_inc(c2_mm, 1)
                elif j in (3, 5):
                    half = (j - 3) // 2
                    pe.wait_ge(P2_ready, T)
                    last = power(P3_bank(0), 0, (2 * half, 2 * half + 1), P2_hi, P2_lo)
                    if half:
                        last.then_inc(P3_mm, 1)
            pe.wait_ge(c2_ready, 1)
            power(P3_bank(1), 1, range(T), P2_hi, P2_lo).then_inc(P3_mm, 1)
            power(P3_bank(2), 2, range(0, 2), P2_hi, P2_lo)

            def y_nodes(c, s, later=True):
                pe.wait_ge(y_ready, c + 1)
                pe.wait_ge(r_ready, c + 1)
                if later:
                    pe.wait_ge(U_split, c * 3)
                for t in range(T):
                    last = pe.transpose(bank[0][:, t * P:(t + 1) * P], y_T[:, s % 2, t * P:(t + 1) * P], ident[:])
                last.then_inc(y_tr, 1)

            def powers_of_x(c, s, nxt=True, later=True):
                if later:
                    pe.wait_ge(x1_split, c + 1)
                for j, (m_hi, m_lo) in enumerate(((PT_hi, PT_lo), (P2_hi, P2_lo))):
                    pe.wait_ge(U_split, c * 3 + (j + 1))
                    if j == 1 and later:
                        pe.wait_ge(Z_stored, c * T)
                    if not later and j == 1:
                        pe.wait_ge(P3_ready, 3)
                    for t in range(T):
                        if not later and j == 0:
                            pe.wait_ge(x1_lo_first, c * T + t + 1)
                        k = slice(t * D, (t + 1) * D)
                        last = split_mm(bank[2 + j], x1_hi[:, s % 2, k], x1_lo[:, s % 2, k], m_hi[:, t],
                                        m_lo[:, t], t == 0, t == T - 1)
                    last.then_inc(U_done, 1)
                if later:
                    pe.wait_ge(r_ready, c + (3 if nxt else 2))
                else:
                    pe.wait_ge(U_split, c * 3 + 3)
                for t in range(T):
                    last = pe.transpose(U_bank(0, later)[:, t * P:(t + 1) * P], X[:, s % 4, t * D:(t + 1) * D],
                                        ident[:])
                last.then_inc(U_done, 1)

            def stage_u(c, s, nxt=True):
                if nxt:
                    y_nodes(c + 1, s + 1)
                powers_of_x(c, s, nxt)

            def stage_z(c, s, nxt=True):
                pe.wait_ge(U_split, c * 3 + 6)
                for t in range(T):
                    pe.wait_ge(Z_stored, c * T + (t + 1))
                    if t == 3 and nxt:
                        pe.wait_ge(U_split, c * 3 + 8)
                    k = slice(t * P, (t + 1) * P)
                    for j in range(3):
                        last = split_mm(Z_bank(t)[:, 0:3 * D], UT_hi[:, s % 2, j, k], UT_lo[:, s % 2, j, k],
                                        G_hi[:, j].rearrange("p a d -> p (a d)"),
                                        G_lo[:, j].rearrange("p a d -> p (a d)"), j == 0, j == 2)
                    last.then_inc(Z_done, 1)

            def times_p3(hi, lo, t, parts, part_ready, need, done):
                for u in parts:
                    pe.wait_ge(part_ready, need(u))
                    k = slice(t * P, (t + 1) * P)
                    last = split_mm(bank[6 + t % 2], P3_hi[:, u, k], P3_lo[:, u, k], hi(u), lo(u), u == 0, u == T - 1)
                if T - 1 in parts:
                    last.then_inc(done, 1)

            P3_STEPS = ((0, (0, 1, 2)), (1, (0, 1)), (0, (3,)), (1, (2, 3)), (2, range(T)), (3, range(T)))

            def stage_v(g, end=False):
                for t, parts in P3_STEPS:
                    if t >= 2:
                        pe.wait_ge(V_sum, g * T + (t - 1))
                    else:
                        pe.wait_ge(q_ready, g * T + 1)
                    times_p3(lambda u: Z2_hi[:, u].rearrange("p s d -> p (s d)"),
                             lambda u: Z2_lo[:, u].rearrange("p s d -> p (s d)"), t, parts, Z2_split,
                             lambda u: g * GB + (GB + (u if end else 0)), V_done)

            def stage_f(g):
                for t, parts in P3_STEPS:
                    if t >= 2:
                        pe.wait_ge(q_ready, g * T + t)
                    else:
                        pe.wait_ge(V_sum, g * T + (t + 3))
                    times_p3(lambda u: V_hi[:, u], lambda u: V_lo[:, u], t, parts, V_split,
                             lambda u: g * T + (u + 1), F_done)

            pe.wait_ge(bn2_ready, 1)
            pe.wait_ge(P3_ready, 1)
            y_nodes(0, 0, later=False)
            power(P3_bank(2), 2, range(2, T), P2_hi, P2_lo).then_inc(P3_mm, 1)
            power(P3_bank(3), 3, range(T), P2_hi, P2_lo).then_inc(P3_mm, 1)
            y_nodes(1, 1, later=False)
            pe.wait_ge(P3_ready, 2)
            powers_of_x(0, 0, later=False)
            y_nodes(2, 2, later=False)
            powers_of_x(1, 1, later=False)
            pe.wait_ge(G_ready, 1)
            pe.wait_ge(P3_ready, T)
            with pe.Fori(0, NG - 1) as g:
                for s in range(GB):
                    stage_z(g * GB + s, s)
                    stage_u(g * GB + (s + 2), s + 2)
                stage_v(g)
                stage_f(g)
            g = NG - 1
            for s in range(GB):
                stage_z(g * GB + s, s, nxt=s < GB - 1)
                if s < 2:
                    stage_u(g * GB + s + 2, s + 2, nxt=s < 1)
            stage_v(g, end=True)
            stage_f(g)


_ORDER = ["x", "adj", "L0_gnn_W1", "L0_gnn_b1", "L0_gnn_g1", "L0_gnn_be1", "L0_gnn_W2", "L0_gnn_b2", "L0_gnn_g2",
          "L0_gnn_be2", "L1_gnn_alpha_train", "L1_gnn_w", "L1_gnn_d", "L1_gnn_fc_in_w", "L1_gnn_fc_in_b"]


def kernel(**inputs):
    import numpy as _np
    import concourse.bacc as _bacc
    from concourse import mybir as _mybir
    from concourse.bass_utils import run_bass_kernel_spmd as _run

    nc = _bacc.Bacc("TRN2", target_bir_lowering=False, num_devices=1)
    arrays, args = {}, []
    for name in _ORDER:
        a = _np.ascontiguousarray(inputs[name])
        arrays[f"in_{name}"] = a
        args.append(nc.dram_tensor(f"in_{name}", a.shape, _mybir.dt.from_np(a.dtype), kind="ExternalInput").ap())
    o = nc.dram_tensor("out_0", inputs["x"].shape, F32, kind="ExternalOutput").ap()
    gnn_kernel(nc, *args, o)
    r = _run(nc, [arrays], core_ids=[0])
    return r.results[0]["out_0"]
```
